# Optimizing a Trainium2 kernel written in Bass

```python
import numpy as np
import jax
import jax.numpy as jnp

def _softmax(x, axis=-1):
    return jax.nn.softmax(x, axis=axis)

def _gelu(x):
    return jax.nn.gelu(x, approximate=True)

def _silu(x):
    return jax.nn.silu(x)

def _sigmoid(x):
    return jax.nn.sigmoid(x)

def _layernorm(x, axis=-1, eps=1e-05):
    m = jnp.mean(x, axis=axis, keepdims=True)
    v = jnp.var(x, axis=axis, keepdims=True)
    return (x - m) / jnp.sqrt(v + eps)

def _scatter_add(tgt, idx, src, axis=0):
    return tgt.at[idx].add(src)

def _segment_sum(src, seg, n):
    return jax.ops.segment_sum(src, seg, n)
kernel_name = 'mk_adaln_ffn_d1_seqx_r4_873278'

def setup_inputs(seed: int=0):
    np.random.seed(seed)
    _w = jnp.asarray

    def _rec_inputs():
        import jax
        import jax.numpy as jnp
        _rk = jax.random.key(seed)
        x = -0.000125 + 0.9999 * jax.random.normal(jax.random.fold_in(_rk, 1), (128, 64, 1024), jnp.float32)
        _lenS = 64 - jax.random.randint(jax.random.fold_in(_rk, 7), (128,), 0, max(1, 64 // 4) + 1, jnp.int32)
        _lenS2 = 64 - jax.random.randint(jax.random.fold_in(_rk, 8), (128,), 0, max(1, 64 // 4) + 1, jnp.int32)
        cond_128 = 0.0061147 + 1.02565 * jax.random.normal(jax.random.fold_in(_rk, 11), (128, 128), jnp.float32)
        fside_S_0 = -0.022604 + 0.987366 * jax.random.normal(jax.random.fold_in(_rk, 12), (64,), jnp.float32)
        return (x, cond_128, fside_S_0)
    x, cond_128, fside_S_0 = _rec_inputs()

    def _L0_cond_setup():
        import jax, jax.numpy as jnp
        import numpy as np
        from jax import lax
        N, C_IN, L = (32, 64, 1024)
        C_OUT, K, GROUPS = (64, 9, 4)
        C_DIM, PAD, STRIDE = (128, 4, 1)
        key = jax.random.key(seed)
        k1, k2, k3, k4, k5 = jax.random.split(key, 5)
        x = jax.random.normal(k1, (N, C_IN, L), dtype=jnp.float32)
        c = jax.random.normal(k2, (N, C_DIM), dtype=jnp.float32)
        weight = jax.random.normal(k3, (C_OUT, C_IN // GROUPS, K), dtype=jnp.float32)
        c_weight = jax.random.normal(k4, (C_OUT, C_DIM), dtype=jnp.float32)
        bias = jax.random.normal(k5, (C_OUT,), dtype=jnp.float32)
        return {'x': x, 'c': c, 'weight': weight, 'c_weight': c_weight, 'bias': bias}
    _L0_cond_all = _L0_cond_setup()
    _L0_cond_in = {k: v for k, v in _L0_cond_all.items() if k in ('weight', 'c_weight')}
    del _L0_cond_all

    def _L0_ffn_setup():
        import jax, jax.numpy as jnp
        import numpy as np
        B, L, H, Dh, M = (4, 512, 16, 64, 256)
        D = H * Dh
        key = jax.random.key(seed)
        kx, ku, kd, kp = jax.random.split(key, 4)
        x = jax.random.normal(kx, (B, L, D), dtype=jnp.float32)
        up = jax.random.normal(ku, (H, Dh, M), dtype=jnp.float32)
        down = jax.random.normal(kd, (H, M, Dh), dtype=jnp.float32)
        perm = jax.random.permutation(kp, D)
        return {'x': x, 'up': up, 'down': down, 'perm': perm}
    _L0_ffn_all = _L0_ffn_setup()
    _L0_ffn_in = {k: v for k, v in _L0_ffn_all.items() if k in ('up', 'down', 'perm')}
    del _L0_ffn_all
    return {'x': x, 'cond_128': cond_128, 'fside_S_0': fside_S_0, 'L0_cond_weight': _L0_cond_in['weight'], 'L0_cond_c_weight': _L0_cond_in['c_weight'], 'L0_ffn_up': _L0_ffn_in['up'], 'L0_ffn_down': _L0_ffn_in['down'], 'L0_ffn_perm': _L0_ffn_in['perm']}

def reference(x, cond_128, fside_S_0, L0_cond_weight, L0_cond_c_weight, L0_ffn_up, L0_ffn_down, L0_ffn_perm):
    import jax
    import jax.numpy as jnp

    def _L0_cond_ref(x, c, weight, c_weight, bias):
        import jax, jax.numpy as jnp
        import numpy as np
        from jax import lax
        N, C_IN, L = (32, 64, 1024)
        C_OUT, K, GROUPS = (64, 9, 4)
        C_DIM, PAD, STRIDE = (128, 4, 1)
        out = lax.conv_general_dilated(x, weight, window_strides=(STRIDE,), padding=[(PAD, PAD)], dimension_numbers=('NCH', 'OIH', 'NCH'), feature_group_count=GROUPS)
        ctx = jnp.einsum('nd,od->no', c, c_weight)
        out = out + ctx[:, :, None] + bias[None, :, None]
        return out

    def _L0_ffn_ref(x, up, down, perm):
        import jax, jax.numpy as jnp
        import numpy as np
        B, L, H, Dh, M = (4, 512, 16, 64, 256)
        D = H * Dh
        b, l, Dm = x.shape
        h, d = (up.shape[0], up.shape[1])
        unperm = jnp.argsort(perm)
        t = x.reshape(b * l, Dm)
        t = t[:, perm]
        t = t.reshape(b * l, h, d)
        t = jnp.einsum('bhd,hdm->bhm', t, up)
        t = jax.nn.gelu(t, approximate=False)
        t = jnp.einsum('bhm,hmd->bhd', t, down)
        t = t.reshape(b * l, h * d)
        t = t[:, unperm]
        out = t.reshape(b, l, Dm)
        return out
    x = x + _L0_ffn_ref(_L0_cond_ref(x, cond_128, L0_cond_weight, L0_cond_c_weight, fside_S_0), L0_ffn_up, L0_ffn_down, L0_ffn_perm)
    return x

_drawn_inputs = setup_inputs


def setup_inputs(seed=0):
    import zlib

    import numpy as np

    out = dict(_drawn_inputs(seed))
    spreads = {}
    factors = {}
    for name, (base, spread) in spreads.items():
        noise = np.random.default_rng([zlib.crc32(name.encode()), seed]).standard_normal(out[name].shape)
        drawn = base * np.exp(spread * noise) if base else spread * noise
        out[name] = jnp.asarray(drawn.astype(out[name].dtype))
    for name, factor in factors.items():
        out[name] = (out[name] * factor).astype(out[name].dtype)
    return out
```

```python
import concourse.bass as bass
from concourse import mybir
from contextlib import ExitStack

F32 = mybir.dt.float32
F32R = mybir.dt.float32r
I32 = mybir.dt.int32
ALU = mybir.AluOpType
ACT = mybir.ActivationFunctionType


class Count:

    def __init__(self, now, least):
        self.now, self.least = now, least

    def __add__(self, k):
        return Count(self.now + k, self.least + k)

    def __sub__(self, k):
        return self + (-k)

    def __mul__(self, k):
        return Count(self.now * k, self.least * k)

    def __floordiv__(self, k):
        return Count(self.now // k, self.least // k)

    def __mod__(self, k):
        return Count(self.now % k, self.least % k)


def adaln_ffn_kernel(nc, x, cond, bias, conv_w, cond_w, up, down, perm, out):
    N, C, L = x.shape
    G, TAPS, CI = 4, conv_w.shape[2], conv_w.shape[1]
    CD = cond.shape[1]
    H, D, M = up.shape
    CO = C // G
    J = 8
    PAD = TAPS // 2
    P = 128
    LC = 128
    NB = LC // J
    XW = LC + J
    CHUNKS = L // LC
    UNITS = G * CHUNKS
    STEPS = 4
    COLS = 512
    OH = CO // 2
    ROW = OH * N
    KT = M // P
    GP = L - LC
    FFN_LAG = CHUNKS + 1
    FIN_LAG = 2 * FFN_LAG
    assert (N, C, CI, CO, M, D) == (P, G * CO, 16, 16, 2 * P, P // 2) and CHUNKS == 8 == H // 2

    y_dram = nc.dram_tensor("y_dram", [G * L * 2, ROW], F32, kind="Internal").ap()
    z_dram = nc.dram_tensor("z_dram", [G * L * 2, ROW], F32, kind="Internal").ap()

    ctx = ExitStack()
    with ctx:
        def sb(name, shape, dt=F32):
            return ctx.enter_context(nc.sbuf_tensor(name, shape, dt))

        def sem(name):
            return ctx.enter_context(nc.semaphore(name))

        ident = sb("ident", [P, P])
        tap_in = sb("tap_in", [C, CI, TAPS])
        tap_row = sb("tap_row", [C, 3 * J, CI])
        cw_rep = sb("cw_rep", [P, G, CD])
        cwT = sb("cwT", [P, G, P])
        c_row = sb("c_row", [N, CD])
        cT = sb("cT", [CD, N])
        bias_rep = sb("bias_rep", [P, G])
        ctx_bias = sb("ctx_bias", [P, G, N])
        conv_all = sb("conv_all", [P, G, 2, 2, P], F32R)
        conv_st = sb("conv_st", [P, 2, 2, 2, P], F32R)
        up_raw = sb("up_raw", [P, 2, M])
        up_all = sb("up_all", [P, H, 2, M], F32R)
        up_st = sb("up_st", [P, 2, 2, 2, M], F32R)
        down_all = sb("down_all", [P, H, KT, D])
        down_st = sb("down_st", [P, 2, 2, KT, D])
        perm_g = sb("perm_g", [P, H], I32)
        perm_s = sb("perm_s", [P, CHUNKS], I32)
        rows_all = sb("rows_all", [P, UNITS, 6], I32)
        rows_g = sb("rows_g", [P, 2, 4], I32)
        rows_s = sb("rows_s", [P, 2, 2], I32)
        x_in = sb("x_in", [N, 2, CI, XW])
        x_ord = sb("x_ord", [N, 2, 5, J * CI])
        xT_hi = sb("xT_hi", [P, NB + 1, N], F32R)
        xT_lo = sb("xT_lo", [P, NB + 1, N], F32R)
        y_sb = sb("y_sb", [P, STEPS, COLS])
        t_in = sb("t_in", [P, 2, 2, ROW])
        t_st = sb("t_st", [P, 2, 2, COLS], F32R)
        h_sb = sb("h_sb", [P, 2, 2, KT, COLS])
        z_sb = sb("z_sb", [P, 2, ROW])
        zt_in = sb("zt_in", [P, 2, OH, N])
        x_res = sb("x_res", [N, 2, OH, LC])

        ps = ctx.enter_context(nc.psum_tensor("ps", [P, 8, COLS], F32))
        UP_BANK = (0, 2)
        xT_ps, conv_ps, down_ps, fin_ps = (ps[:, b, :] for b in (4, 5, 6, 7))

        const_loaded, perm_loaded = sem("const_loaded"), sem("perm_loaded")
        up_loaded = [sem(f"up_loaded{k}") for k in range(2)]
        down_loaded = sem("down_loaded")
        ident_made, pad_zero, prep_pe, prep_dve = (sem(n) for n in ("ident_made", "pad_zero", "prep_pe", "prep_dve"))
        taps_laid = sem("taps_laid")
        up_split, rows_made = sem("up_split"), sem("rows_made")
        x_loaded = [sem(f"x_loaded{k}") for k in range(2)]
        xT_done, hi_done, lo_done, lo_raw = sem("xT_done"), sem("hi_done"), sem("lo_done"), sem("lo_raw")
        x_ordered = sem("x_ordered")
        conv_done, y_done = sem("conv_done"), sem("y_done")
        y_stored = [sem(f"y_stored{s}") for s in range(STEPS)]
        conv_staged, ffn_staged = sem("conv_staged"), sem("ffn_staged")
        pool_passed = sem("pool_passed")
        rows_g_done, rows_s_done = sem("rows_g_done"), sem("rows_s_done")
        gathered = [sem(f"gathered{k}") for k in range(2)]
        t_hi_done, t_split = sem("t_hi_done"), sem("t_split")
        up_done, gelu_done, down_done, z_done = sem("up_done"), sem("gelu_done"), sem("down_done"), sem("z_done")
        scattered = [sem(f"scattered{k}") for k in range(2)]
        zt_loaded = [sem(f"zt_loaded{k}") for k in range(2)]
        res_loaded = [sem(f"res_loaded{k}") for k in range(2)]
        fin_done, sum_done = sem("fin_done"), sem("sum_done")
        out_stored = [sem(f"out_stored{k}") for k in range(2)]

        def hold(eng, what, count):
            if count.least > 0:
                eng.wait_ge(what, count.now)

        def units(t, s=0):
            return t + s // STEPS, t + (s // STEPS - FFN_LAG), t + (s // STEPS - FIN_LAG), s % STEPS

        def live(unit, least=0):
            return least <= unit.least < UNITS

        LAST = UNITS + FIN_LAG + 1

        def pipeline(eng, iteration, by_group=False):
            def kind(i):
                t0 = 2 * i
                return (by_group and i // (CHUNKS // 2),) + tuple(
                    min(max(t0 - lag, -3) // 2 * 2, 4) if t0 - lag < UNITS - 2 else 10 + min(t0 - lag - UNITS, 3)
                    for lag in (0, FFN_LAG + 1, FIN_LAG))
            i, end = 0, (LAST + 2) // 2
            while i < end:
                n = i + 1
                while n < end and kind(n) == kind(i):
                    n += 1
                if n - i == 1:
                    for k in range(2):
                        iteration(Count(2 * i + k, 2 * i + k), k)
                else:
                    with eng.Fori(i, n) as r:
                        for k in range(2):
                            iteration(Count(r * 2 + k, 2 * i + k), k)
                i = n

        def position_of(unit):
            return unit.now * LC + (unit // CHUNKS).now * (CO * L - L)

        block = ctx.enter_context(nc.Block())

        @block.sync
        def _(sp):
            def x_window(first, cols):
                return bass.AP(x.tensor, first, [[C * L, N], [L, CI], [1, cols]])

            with nc.allow_non_contiguous_dma(reason="small tables of the prologue"):
                sp.dma_start(tap_in[:, :, :], conv_w).then_inc(const_loaded, 16)
                sp.dma_start(c_row[:, :], cond).then_inc(const_loaded, 16)
                for j in range(J):
                    rows = slice(j * CO, (j + 1) * CO)
                    sp.dma_start(cw_rep[rows, :, :], cond_w.rearrange("(g o) d -> o g d", g=G)).then_inc(const_loaded, 16)
                    sp.dma_start(bias_rep[rows, :], bias.rearrange("(g o) -> o g", g=G)).then_inc(const_loaded, 16)
                sp.dma_start(x_in[:, 0, :, PAD:XW], x_window(0, XW - PAD)).then_inc(x_loaded[0], 16)
                for b in range(2):
                    sp.dma_start(perm_g[b * D:(b + 1) * D, :], perm.rearrange("(h d) -> d h", d=D)).then_inc(perm_loaded, 16)
                sp.dma_start(perm_s[:, :], perm.rearrange("(p d) -> d p", d=P)).then_inc(perm_loaded, 16)
                sp.dma_start(down_all[:, :, :, :], down.rearrange("h (k m) d -> m h k d", k=KT)).then_inc(down_loaded, 16)

            def iteration(t, k):
                for s in range(STEPS):
                    if s == 0:
                        cv = t + 1
                        if live(cv):
                            x_at = position_of(cv) - PAD
                            hold(sp, x_ordered, (cv - 1) * STEPS)
                            par = (k + 1) % 2
                            if t.least == UNITS - 2:
                                sp.dma_start(x_in[:, par, :, 0:XW - PAD],
                                             x_window(x_at, XW - PAD)).then_inc(x_loaded[par], 16)
                            else:
                                sp.dma_start(x_in[:, par, :, :],
                                             x_window(x_at, XW)).then_inc(x_loaded[par], 16)
                    cv, _, _, q = units(t, s - 1)
                    if live(cv):
                        at = cv.now * (LC * 2 * ROW)
                        sp.wait_ge(y_done, (cv * STEPS + q + 1).now)
                        dst = bass.AP(y_dram.tensor, at + q * (COLS // N * J * 2 * ROW),
                                      [[N, P], [J * 2 * ROW, COLS // N], [1, N]])
                        sp.dma_start(dst, y_sb[:, q, :].rearrange("p (b n) -> p b n", n=N)).then_inc(y_stored[q], 16)
                    if s in (1, 3):
                        half = 1 if s == 1 else 0
                        _, _, fin, _ = units(t, 0 if s == 1 else STEPS)
                        if live(fin):
                            z_at = fin.now * (LC * 2 * ROW) + half * ROW
                            x_at = position_of(fin) + half * (OH * L)
                            hold(sp, fin_done, fin * STEPS - (STEPS - 2 * half - 2))
                            for b in range(2):
                                sp.wait_ge(scattered[b], ((fin // CHUNKS) * (16 * CHUNKS) + 16 * CHUNKS).now)
                            src = bass.AP(z_dram.tensor, z_at, [[2 * ROW, P], [1, ROW]])
                            sp.dma_start(zt_in[:, half, :, :].rearrange("p o n -> p (o n)"), src).then_inc(zt_loaded[half], 16)
                            hold(sp, out_stored[half], fin * 16)
                            src = bass.AP(x.tensor, x_at, [[C * L, N], [L, OH], [1, LC]])
                            sp.dma_start(x_res[:, half, :, :], src).then_inc(res_loaded[half], 16)

            pipeline(sp, iteration)
            for b in range(2):
                sp.wait_ge(out_stored[b], 16 * UNITS)

        @block.gpsimd
        def _(pool):
            nc.gpsimd.memset(ident[:, :], 0.0).then_inc(ident_made, 1)
            pool.wait_ge(ident_made, 1)
            nc.gpsimd.affine_select(out=ident[:, :], in_=ident[:, :], compare_op=ALU.not_equal, fill=1.0, base=0,
                                    pattern=[[-1, P]], channel_multiplier=1).then_inc(ident_made, 1)

            def pass_waits():
                pool.sem_inc(pool_passed, 1)

            def iteration(t, k):
                cv, ffn, _, _ = units(t)
                if live(ffn - 1):
                    scatter(ffn - 1, (k + FFN_LAG + 1) % 2, 1)
                if live(cv + 1):
                    stage_conv(cv + 1, (k + 1) % 2)
                if live(ffn + 1):
                    par = (k + FFN_LAG + 1) % 2
                    stage_ffn(ffn + 1, par)
                    gather(ffn + 1, par, 0)
                if live(ffn):
                    par = (k + FFN_LAG) % 2
                    src = rows_of(ffn)[:, 4:6]
                    pool.wait_ge(rows_made, 1)
                    for b in range(2):
                        hold(pool, scattered[b], (ffn - 1) * 16)
                    pass_waits()
                    nc.gpsimd.tensor_copy(rows_s[:, par, :], src).then_inc(rows_s_done, 1)
                    scatter(ffn, par, 0)
                if live(ffn + 1):
                    gather(ffn + 1, (k + FFN_LAG + 1) % 2, 1)

            def rows_of(ffn):
                return columns(rows_all[:, :, :].rearrange("p u w -> p (u w)"), ffn.now * 6, 6)

            def columns(flat, first, n):
                return flat[:, bass.ds(first, n)]

            def stage_conv(cv, par):
                W = 4 * P
                src = columns(conv_all[:, :, :, :, :].rearrange("p g a b m -> p (g a b m)"), (cv // CHUNKS).now * W, W)
                dst = conv_st[:, par, :, :, :].rearrange("p a b m -> p (a b m)")
                pool.wait_ge(prep_dve, 2)
                hold(pool, conv_done, (cv - 1) * STEPS)
                pass_waits()
                nc.gpsimd.tensor_copy(dst, src).then_inc(conv_staged, 1)

            def stage_ffn(ffn, par):
                pair = (ffn % CHUNKS).now
                W = 4 * M
                up_src = columns(up_all[:, :, :, :].rearrange("p h a m -> p (h a m)"), pair * W, W)
                W = 2 * KT * D
                down_src = columns(down_all[:, :, :, :].rearrange("p h k d -> p (h k d)"), pair * W, W)
                pool.wait_ge(up_split, H)
                hold(pool, down_done, (ffn - 1) * STEPS)
                pass_waits()
                nc.gpsimd.tensor_copy(up_st[:, par, :, :, :].rearrange("p h a m -> p (h a m)"), up_src)
                pool.wait_ge(down_loaded, 16)
                nc.gpsimd.tensor_copy(down_st[:, par, :, :, :].rearrange("p h k d -> p (h k d)"), down_src).then_inc(ffn_staged, 1)
                src = rows_of(ffn)[:, 0:4]
                pool.wait_ge(rows_made, 1)
                for b in range(2):
                    hold(pool, gathered[b], (ffn - 1) * 32)
                pass_waits()
                nc.gpsimd.tensor_copy(rows_g[:, par, :], src).then_inc(rows_g_done, 1)

            def gather(ffn, par, half):
                hold(pool, rows_g_done, ffn + 1)
                for s in range(STEPS):
                    hold(pool, y_stored[s], (ffn // CHUNKS) * (16 * CHUNKS) + 16 * CHUNKS)
                hold(pool, t_split, ffn * STEPS - (STEPS - 2 * half - 2))
                pass_waits()
                table = y_dram[0:(ffn.least // CHUNKS + 1) * L * 2, :]
                for head in range(2):
                    w = 2 * half + head
                    nc.gpsimd.indirect_dma_start(
                        out=t_in[:, half, head, :], out_offset=None, in_=table,
                        in_offset=bass.IndirectOffsetOnAxis(ap=rows_g[:, par, w:w + 1], axis=0),
                    ).then_inc(gathered[half], 16)

            def scatter(ffn, par, half):
                hold(pool, rows_s_done, ffn + 1)
                hold(pool, z_done, ffn * STEPS + 2 * half + 2)
                pass_waits()
                nc.gpsimd.indirect_dma_start(
                    out=z_dram, in_=z_sb[:, half, :], in_offset=None,
                    out_offset=bass.IndirectOffsetOnAxis(ap=rows_s[:, par, half:half + 1], axis=0),
                ).then_inc(scattered[half], 16)

            stage_conv(Count(0, 0), 0)
            pipeline(pool, iteration, by_group=True)

        @block.scalar
        def _(act):
            for p in range(H // 2):
                if p:
                    act.wait_ge(up_split, 2 * p)
                for b in range(2):
                    act.dma_start(up_raw[b * D:(b + 1) * D, :, :],
                                  up[2 * p:2 * p + 2, :, :].rearrange("h d m -> d h m")).then_inc(up_loaded[b], 16)

            def iteration(t, k):
                for s in range(STEPS):
                    cv, ffn, _, _ = units(t)
                    if live(cv):
                        act.wait_ge(xT_done, (cv * STEPS + s + 1).now)
                        if s == 0:
                            nc.scalar.activation(xT_hi[:, 0, :], fin_ps[:, 0:N], ACT.Copy)
                        nc.scalar.activation(xT_hi[:, 4 * s + 1:4 * s + 5, :].rearrange("p b n -> p (b n)"), xT_ps,
                                             ACT.Copy).then_inc(hi_done, 1)
                    if live(ffn):
                        for head in range(2):
                            act.wait_ge(up_done, (ffn * (2 * STEPS) + 2 * s + head + 1).now)
                            hold(act, down_done, ffn * STEPS + s - 1)
                            nc.scalar.activation(h_sb[:, s % 2, head, :, :], ps[:, UP_BANK[head]:UP_BANK[head] + 2, :],
                                                 ACT.Gelu).then_inc(gelu_done, 1)
                    _, ffn, _, q = units(t, s - 1)
                    if live(ffn):
                        act.wait_ge(down_done, (ffn * STEPS + q + 1).now)
                        if q % 2 == 0:
                            hold(act, scattered[q // 2], ffn * 16)
                        nc.scalar.activation(z_sb[:, q // 2, (q % 2) * COLS:(q % 2 + 1) * COLS], down_ps,
                                             ACT.Copy).then_inc(z_done, 1)
                    cv, _, _, q = units(t, s + 1)
                    if live(cv):
                        order(cv, (k + (s + 1) // STEPS) % 2, q)
                    _, _, fin, q = units(t, s - 1)
                    if live(fin) and q % 2 == 1:
                        half = q // 2
                        act.wait_ge(sum_done, (fin * STEPS + q + 1).now)
                        dst = bass.AP(out.tensor, position_of(fin) + half * (OH * L), [[C * L, N], [L, OH], [1, LC]])
                        act.dma_start(dst, x_res[:, half, :, :]).then_inc(out_stored[half], 16)

            def order(cv, par, s):
                if s == 0:
                    act.wait_ge(x_loaded[par], ((cv // 2) * 16 + 16).now)
                hold(act, xT_done, cv * STEPS + s - 1)
                b = 0 if s == 0 else 1
                src = x_in[:, par, :, (4 * s + b) * J:(4 * s + 5) * J].rearrange("n i (b j) -> n b j i", j=J)
                dst = x_ord[:, s % 2, b:5, :].rearrange("n b (j i) -> n b j i", j=J)
                nc.scalar.activation(dst, src, ACT.Copy).then_inc(x_ordered, 1)

            act.wait_ge(pad_zero, 1)
            order(Count(0, 0), 0, 0)
            pipeline(act, iteration)

        @block.vector
        def _(dve):
            nc.vector.memset(x_in[:, 0, :, 0:PAD], 0.0).then_inc(pad_zero, 1)
            nc.vector.memset(tap_row[:, 0:J, :], 0.0)
            nc.vector.memset(tap_row[:, J + TAPS:3 * J, :], 0.0)
            dve.wait_ge(const_loaded, 16 * (2 + 2 * J))
            nc.vector.tensor_copy(tap_row[:, J:J + TAPS, :], tap_in[:, :, :].rearrange("c i t -> c t i")).then_inc(taps_laid, 1)
            dve.wait_ge(perm_loaded, 48)
            for g in range(G):
                for half in range(2):
                    us = slice(g * CHUNKS, (g + 1) * CHUNKS)
                    nc.vector.tensor_scalar(rows_all[:, us, 2 * half:2 * half + 2],
                                            perm_g[:, :].rearrange("p (u h) -> p u h", h=2),
                                            2, 2 * g * L + half, ALU.mult, ALU.add)
                    last = nc.vector.tensor_scalar(rows_all[:, us, 4 + half], perm_s[:, :],
                                                   2, 2 * g * L + half, ALU.mult, ALU.add)
            last.then_inc(rows_made, 1)
            dve.wait_ge(prep_pe, 1)
            for kt in range(2):
                src = ps[:, 2 * kt:2 * kt + 2, :].rearrange("p a w -> p (a w)")[:, 0:J * C]
                src = src.rearrange("p (j g o) -> p g j o", j=J, g=G)
                for g in range(G):
                    hi = conv_all[:, g, 0, kt, :].rearrange("p (j o) -> p j o", j=J)
                    last = nc.vector.tensor_copy(hi, src[:, g, :, :])
            last.then_inc(prep_dve, 1)
            dve.wait_ge(prep_dve, 1)
            for kt in range(2):
                src = ps[:, 2 * kt:2 * kt + 2, :].rearrange("p a w -> p (a w)")[:, 0:J * C]
                src = src.rearrange("p (j g o) -> p g j o", j=J, g=G)
                for g in range(G):
                    hi = conv_all[:, g, 0, kt, :].rearrange("p (j o) -> p j o", j=J)
                    lo = conv_all[:, g, 1, kt, :].rearrange("p (j o) -> p j o", j=J)
                    last = nc.vector.tensor_tensor(lo, src[:, g, :, :], hi.bitcast(F32), ALU.subtract)
            last.then_inc(prep_dve, 1)
            dve.wait_ge(prep_pe, 2)
            nc.vector.tensor_copy(cwT[:, :, :].rearrange("p g m -> p (g m)"), ps[:, 4, :])
            nc.vector.tensor_copy(cT[:, :], ps[:, 5, 0:N]).then_inc(prep_dve, 1)
            dve.wait_ge(prep_pe, 3)
            for g in range(G):
                last = nc.vector.tensor_scalar(ctx_bias[:, g, :], ps[:, 6, g * N:(g + 1) * N], bias_rep[:, g:g + 1], None,
                                               ALU.add)
            last.then_inc(prep_dve, 1)
            for p in range(H // 2):
                for b in range(2):
                    dve.wait_ge(up_loaded[b], 16 * (p + 1))
                hs = slice(2 * p, 2 * p + 2)
                nc.vector.tensor_copy(up_all[:, hs, 0, :], up_raw[:, :, :]).then_inc(up_split, 1)
                dve.wait_ge(up_split, 2 * p + 1)
                nc.vector.tensor_tensor(up_all[:, hs, 1, :], up_raw[:, :, :], up_all[:, hs, 0, :].bitcast(F32),
                                        ALU.subtract).then_inc(up_split, 1)

            def iteration(t, k):
                for s in range(STEPS):
                    cv, _, fin, q = units(t, s - 1)
                    if live(cv):
                        dve.wait_ge(conv_done, (cv * STEPS + q + 1).now)
                        hold(dve, y_stored[q], cv * 16)
                        at = (cv // CHUNKS).now * N
                        add = ctx_bias[:, :, :].rearrange("p g n -> p (g n)")[:, bass.ds(at, N)]
                        nc.vector.tensor_tensor(y_sb[:, q, :].rearrange("p (b n) -> p b n", n=N),
                                                conv_ps.rearrange("p (b n) -> p b n", n=N),
                                                add.unsqueeze(1).to_broadcast([P, COLS // N, N]),
                                                ALU.add).then_inc(y_done, 1)
                    if live(fin):
                        half, o = q // 2, 4 * (q % 2)
                        dve.wait_ge(fin_done, (fin * STEPS + q + 1).now)
                        dve.wait_ge(res_loaded[half], (fin * 16 + 16).now)
                        here = x_res[:, half, o:o + 4, :]
                        nc.vector.tensor_tensor(here, fin_ps.rearrange("p (o l) -> p o l", l=LC), here,
                                                ALU.add).then_inc(sum_done, 1)
                    cv, _, _, _ = units(t)
                    if live(cv):
                        lo_part(cv, s)
                    _, ffn, _, q = units(t, s + 1)
                    if live(ffn):
                        split(ffn, q)

            def lo_part(cv, s):
                dve.wait_ge(hi_done, (cv * STEPS + s + 1).now)

                def lo(b0, b1, src):
                    flat = "p b n -> p (b n)"
                    return nc.vector.tensor_tensor(xT_lo[:, b0:b1, :].rearrange(flat), src,
                                                   xT_hi[:, b0:b1, :].bitcast(F32).rearrange(flat), ALU.subtract)

                def zero_outside(rows, b, block_in_group):
                    def zero():
                        dve.wait_ge(lo_raw, ((cv * 2) + (1 if s == 0 else 2)).now)
                        nc.vector.memset(xT_hi[rows, b, :].bitcast(F32), 0.0)
                        nc.vector.memset(xT_lo[rows, b, :].bitcast(F32), 0.0)

                    place = (cv % CHUNKS).now
                    if isinstance(place, int):
                        if place == block_in_group:
                            zero()
                    else:
                        with dve.If(place == block_in_group):
                            zero()

                if s == 0:
                    lo(0, 1, fin_ps[:, 0:N]).then_inc(lo_raw, 1)
                    zero_outside(slice(0, PAD * CI), 0, 0)
                    lo(1, 5, xT_ps).then_inc(lo_done, 1)
                elif s == 3:
                    lo(NB, NB + 1, xT_ps[:, 3 * N:4 * N]).then_inc(lo_raw, 1)
                    zero_outside(slice(PAD * CI, P), NB, CHUNKS - 1)
                    lo(NB - 3, NB, xT_ps[:, 0:3 * N]).then_inc(lo_done, 1)
                else:
                    lo(4 * s + 1, 4 * s + 5, xT_ps).then_inc(lo_done, 1)

            def split(ffn, q):
                half, cols = q // 2, slice((q % 2) * COLS, (q % 2 + 1) * COLS)
                dve.wait_ge(gathered[half], (ffn * 32 + 32).now)
                hold(dve, up_done, ffn * (2 * STEPS) + 2 * q - 2)
                for head in range(2):
                    nc.vector.tensor_copy(t_st[:, q % 2, head, :], t_in[:, half, head, cols]).then_inc(t_hi_done, 1)
                for head in range(2):
                    dve.wait_ge(t_hi_done, (ffn * (2 * STEPS) + 2 * q + head + 1).now)
                    low = t_st[D:P, q % 2, head, :]
                    last = nc.vector.tensor_tensor(low, t_in[D:P, half, head, cols], low.bitcast(F32), ALU.subtract)
                last.then_inc(t_split, 1)

            pipeline(dve, iteration)

        @block.tensor
        def _(pe):
            pe.wait_ge(ident_made, 2)
            pe.wait_ge(const_loaded, 16 * (2 + 2 * J))
            pe.wait_ge(taps_laid, 1)
            for kt in range(2):
                for j in range(J):
                    src = tap_row[:, (kt + 1) * J - j:(kt + 2) * J - j, :].rearrange("c t i -> c (t i)")
                    last = nc.tensor.transpose(ps[:, 2 * kt, j * C:(j + 1) * C], src, ident[0:C, 0:C])
            last.then_inc(prep_pe, 1)
            for g in range(G):
                nc.tensor.transpose(ps[:, 4, g * P:(g + 1) * P], cw_rep[:, g, :], ident[:, :])
            nc.tensor.transpose(ps[:, 5, 0:N], c_row[:, :], ident[:, :]).then_inc(prep_pe, 1)
            pe.wait_ge(prep_dve, 3)
            for g in range(G):
                last = nc.tensor.matmul(ps[:, 6, g * N:(g + 1) * N], cwT[:, g, :], cT[:, :], start=True, stop=True)
            last.then_inc(prep_pe, 1)
            pe.wait_ge(prep_dve, 4)

            def transpose_x(cv, s):
                pe.wait_ge(x_ordered, (cv * STEPS + s + 1).now)
                hold(pe, lo_done, cv * STEPS + s)
                if s == 0:
                    nc.tensor.transpose(fin_ps[:, 0:N], x_ord[:, 0, 0, :], ident[:, :])
                for b in range(4):
                    last = nc.tensor.transpose(xT_ps[:, b * N:(b + 1) * N], x_ord[:, s % 2, b + 1, :], ident[:, :])
                last.then_inc(xT_done, 1)

            def up_project(ffn, par, s):
                if s == 0:
                    pe.wait_ge(ffn_staged, (ffn + 1).now)
                pe.wait_ge(t_split, (ffn * STEPS + s + 1).now)
                for head in range(2):
                    hold(pe, gelu_done, ffn * (2 * STEPS) + 2 * s + head - 1)
                    for kt in range(KT):
                        for part in range(2):
                            last = nc.tensor.matmul(ps[:, UP_BANK[head] + kt, :],
                                                    up_st[:, par, head, part, kt * P:(kt + 1) * P],
                                                    t_st[:, s % 2, head, :], start=part == 0, stop=part == 1)
                    last.then_inc(up_done, 1)

            def down_project(ffn, par, q):
                pe.wait_ge(gelu_done, (ffn * (2 * STEPS) + 2 * q + 2).now)
                hold(pe, z_done, ffn * STEPS + q)
                for kt in range(KT):
                    for head in range(2):
                        last = nc.tensor.matmul(down_ps[head * D:(head + 1) * D, :], down_st[:, par, head, kt, :],
                                                h_sb[:, q % 2, head, kt, :], start=kt == 0, stop=kt == KT - 1)
                last.then_inc(down_done, 1)

            def finish(fin, cv, s):
                half, o = s // 2, 4 * (s % 2)
                if s % 2 == 0:
                    pe.wait_ge(zt_loaded[half], (fin * 16 + 16).now)
                hold(pe, sum_done, fin * STEPS + s)
                if s == 0 and live(cv):
                    pe.wait_ge(lo_done, (cv * STEPS + 1).now)
                for b in range(4):
                    last = nc.tensor.transpose(fin_ps[:, b * LC:(b + 1) * LC], zt_in[:, half, o + b, :], ident[:, :])
                last.then_inc(fin_done, 1)

            def convolve(cv, par, s):
                if s == 0:
                    pe.wait_ge(conv_staged, (cv + 1).now)
                pe.wait_ge(lo_done, (cv * STEPS + s + 1).now)
                hold(pe, y_done, cv * STEPS + s)
                terms = [(w, part, kt) for w, part in ((0, xT_hi), (0, xT_lo), (1, xT_hi)) for kt in range(2)]
                for n, (w, part, kt) in enumerate(terms):
                    last = nc.tensor.matmul(conv_ps, conv_st[:, par, w, kt, :],
                                            part[:, 4 * s + kt:4 * s + kt + 4, :].rearrange("p b n -> p (b n)"),
                                            start=n == 0, stop=n == len(terms) - 1)
                last.then_inc(conv_done, 1)

            def iteration(t, k):
                cv, ffn, fin, _ = units(t)
                for s in range(STEPS):
                    if live(cv):
                        if s == 0:
                            if live(fin - 1):
                                pe.wait_ge(sum_done, (fin * STEPS).now)
                        transpose_x(cv, s)
                    if live(ffn):
                        up_project(ffn, (k + FFN_LAG) % 2, s)
                    _, prev, _, q = units(t, s - 1)
                    if live(prev):
                        down_project(prev, (k + FFN_LAG + (s == 0)) % 2, q)
                    if live(fin):
                        finish(fin, cv, s)
                    if live(cv):
                        convolve(cv, k, s)

            pipeline(pe, iteration)


_OUT = ((128, 64, 1024), "float32")
_INS = ["x", "cond_128", "fside_S_0", "L0_cond_weight", "L0_cond_c_weight", "L0_ffn_up", "L0_ffn_down", "L0_ffn_perm"]


def kernel(**inputs):
    import numpy as _np
    import concourse.bacc as _bacc
    from concourse import mybir as _mybir
    from concourse.bass_utils import run_bass_kernel_spmd as _run

    nc = _bacc.Bacc("TRN2", target_bir_lowering=False, num_devices=1)
    arrays, args = {}, []
    for name in _INS:
        a = _np.ascontiguousarray(inputs[name])
        arrays[f"in_{name}"] = a
        args.append(nc.dram_tensor(f"in_{name}", a.shape, _mybir.dt.from_np(a.dtype), kind="ExternalInput").ap())
    shape, dtype = _OUT
    args.append(nc.dram_tensor("out_0", shape, _mybir.dt.from_np(_np.dtype(dtype)), kind="ExternalOutput").ap())
    adaln_ffn_kernel(nc, *args)
    r = _run(nc, [arrays], core_ids=[0])
    return r.results[0]["out_0"]
```

```python
import concourse.bass as bass
from concourse import mybir
from contextlib import ExitStack

F32 = mybir.dt.float32
F32R = mybir.dt.float32r
I32 = mybir.dt.int32
ALU = mybir.AluOpType
ACT = mybir.ActivationFunctionType


class Count:

    def __init__(self, now, least):
        self.now, self.least = now, least

    def __add__(self, k):
        return Count(self.now + k, self.least + k)

    def __sub__(self, k):
        return self + (-k)

    def __mul__(self, k):
        return Count(self.now * k, self.least * k)

    def __floordiv__(self, k):
        return Count(self.now // k, self.least // k)

    def __mod__(self, k):
        return Count(self.now % k, self.least % k)


def adaln_ffn_kernel(nc, x, cond, bias, conv_w, cond_w, up, down, perm, out):
    N, C, L = x.shape
    G, TAPS, CI = 4, conv_w.shape[2], conv_w.shape[1]
    CD = cond.shape[1]
    H, D, M = up.shape
    CO = C // G
    J = 8
    PAD = TAPS // 2
    P = 128
    LC = 128
    NB = LC // J
    XW = LC + J
    CHUNKS = L // LC
    UNITS = G * CHUNKS
    STEPS = 4
    COLS = 512
    OH = CO // 2
    ROW = OH * N
    KT = M // P
    FFN_LAG = CHUNKS + 1
    FIN_LAG = 2 * FFN_LAG
    assert (N, C, CI, CO, M, D) == (P, G * CO, 16, 16, 2 * P, P // 2) and CHUNKS == 8 == H // 2

    y_dram = nc.dram_tensor("y_dram", [G * L * 2, ROW], F32, kind="Internal").ap()
    z_dram = nc.dram_tensor("z_dram", [G * L * 2, ROW], F32, kind="Internal").ap()

    ctx = ExitStack()
    with ctx:
        def sb(name, shape, dt=F32):
            return ctx.enter_context(nc.sbuf_tensor(name, shape, dt))

        def sem(name):
            return ctx.enter_context(nc.semaphore(name))

        ident = sb("ident", [P, P])
        tap_in = sb("tap_in", [C, CI, TAPS])
        tap_row = sb("tap_row", [C, 3 * J, CI])
        cw_rep = sb("cw_rep", [P, G, CD])
        cwT = sb("cwT", [P, G, P])
        c_row = sb("c_row", [N, CD])
        cT = sb("cT", [CD, N])
        bias_rep = sb("bias_rep", [P, G])
        ctx_bias = sb("ctx_bias", [P, G, N])
        conv_all = sb("conv_all", [P, G, 2, 2, P], F32R)
        conv_st = sb("conv_st", [P, 2, 2, 2, P], F32R)
        up_raw = sb("up_raw", [P, 2, 2, M])
        up_all = sb("up_all", [P, H, 2, M], F32R)
        up_st = sb("up_st", [P, 2, 2, 2, M], F32R)
        down_all = sb("down_all", [P, H, KT, D])
        down_st = sb("down_st", [P, 2, 2, KT, D])
        perm_sb = sb("perm_sb", [P, CHUNKS], I32)
        rows_all = sb("rows_all", [P, UNITS, 2], I32)
        rows = sb("rows", [P, 2, 2], I32)
        x_in = sb("x_in", [N, 2, CI, XW])
        x_ord = sb("x_ord", [N, 2, 5, J * CI])
        xT_hi = sb("xT_hi", [P, NB + 1, N], F32R)
        xT_lo = sb("xT_lo", [P, NB + 1, N], F32R)
        y_sb = sb("y_sb", [P, STEPS, COLS])
        t_in = sb("t_in", [P, 2, ROW])
        t_st = sb("t_st", [P, 2, 2, COLS], F32R)
        h_sb = sb("h_sb", [P, 2, 2, KT, COLS])
        z_sb = sb("z_sb", [P, 2, ROW])
        zt_in = sb("zt_in", [P, 2, 2, OH, N])
        x_res = sb("x_res", [N, 2, 2, OH, LC])

        ps = ctx.enter_context(nc.psum_tensor("ps", [P, 8, COLS], F32))
        UP_BANK = (0, 2)
        xT_ps, conv_ps, down_ps, fin_ps = (ps[:, b, :] for b in (4, 5, 6, 7))

        taps_loaded, ctx_loaded, bias_loaded, perm_loaded = (
            sem(n) for n in ("taps_loaded", "ctx_loaded", "bias_loaded", "perm_loaded"))
        up_loaded = [sem(f"up_loaded{k}") for k in range(2)]
        down_loaded = sem("down_loaded")
        ident_made, pad_zero, prep_pe, prep_dve = (sem(n) for n in ("ident_made", "pad_zero", "prep_pe", "prep_dve"))
        taps_laid = sem("taps_laid")
        up_split, rows_made = sem("up_split"), sem("rows_made")
        x_loaded = [sem(f"x_loaded{k}") for k in range(2)]
        xT_done, hi_done, lo_done, lo_raw = sem("xT_done"), sem("hi_done"), sem("lo_done"), sem("lo_raw")
        x_ordered = sem("x_ordered")
        conv_done, y_done = sem("conv_done"), sem("y_done")
        y_stored = [sem(f"y_stored{s}") for s in range(STEPS)]
        conv_staged, ffn_staged = sem("conv_staged"), sem("ffn_staged")
        pool_passed = sem("pool_passed")
        rows_done = sem("rows_done")
        gathered = [sem(f"gathered{k}") for k in range(2)]
        t_hi_done, t_split = sem("t_hi_done"), sem("t_split")
        up_done, gelu_done, down_done, z_done = sem("up_done"), sem("gelu_done"), sem("down_done"), sem("z_done")
        scattered = [sem(f"scattered{k}") for k in range(2)]
        zt_loaded = [[sem(f"zt_loaded{par}{half}") for half in range(2)] for par in range(2)]
        res_loaded = [[sem(f"res_loaded{par}{half}") for half in range(2)] for par in range(2)]
        fin_done, sum_done = sem("fin_done"), sem("sum_done")
        out_stored = [[sem(f"out_stored{par}{half}") for half in range(2)] for par in range(2)]

        def hold(eng, what, count):
            if count.least > 0:
                eng.wait_ge(what, count.now)

        def units(t, s=0):
            return t + s // STEPS, t + (s // STEPS - FFN_LAG), t + (s // STEPS - FIN_LAG), s % STEPS

        def live(unit, least=0):
            return least <= unit.least < UNITS

        LAST = UNITS + FIN_LAG + 1

        def pipeline(eng, iteration, by_group=False):
            def kind(i):
                t0 = 2 * i
                return (by_group and i // (CHUNKS // 2),) + tuple(
                    min(max(t0 - lag, -4), 2) if t0 - lag < UNITS - 2 else min(t0 - lag, UNITS + 2)
                    for lag in (0, FFN_LAG + 1, FIN_LAG))
            i, end = 0, (LAST + 2) // 2
            while i < end:
                n = i + 1
                while n < end and kind(n) == kind(i):
                    n += 1
                if n - i == 1:
                    for k in range(2):
                        iteration(Count(2 * i + k, 2 * i + k), k)
                else:
                    with eng.Fori(i, n) as r:
                        for k in range(2):
                            iteration(Count(r * 2 + k, 2 * i + k), k)
                i = n

        def position_of(unit):
            return unit.now * LC + (unit // CHUNKS).now * (CO * L - L)

        block = ctx.enter_context(nc.Block())

        @block.sync
        def _(sp):
            def x_window(first, cols):
                return bass.AP(x.tensor, first, [[C * L, N], [L, CI], [1, cols]])

            def load_up(pair, par):
                src = up.rearrange("h d m -> (h d) m")[bass.ds(pair.now * P, P), :].rearrange("(h d) m -> d h m", d=D)
                for b in range(2):
                    sp.dma_start(up_raw[b * D:(b + 1) * D, par, :, :], src).then_inc(up_loaded[par], 16)

            sp.dma_start(x_in[:, 0, :, PAD:XW], x_window(0, XW - PAD)).then_inc(x_loaded[0], 16)
            sp.dma_start(tap_in[:, :, :], conv_w).then_inc(taps_loaded, 16)
            with nc.allow_non_contiguous_dma(reason="small tables of the prologue"):
                for j in range(J):
                    sp.dma_start(bias_rep[j * CO:(j + 1) * CO, :], bias.rearrange("(g o) -> o g", g=G)).then_inc(bias_loaded, 16)
                sp.dma_start(perm_sb[:, :], perm.rearrange("(p d) -> d p", d=P)).then_inc(perm_loaded, 16)
                sp.dma_start(down_all[:, :, :, :], down.rearrange("h (k m) d -> m h k d", k=KT)).then_inc(down_loaded, 16)

            def iteration(t, k):
                for s in range(STEPS):
                    if s == 0:
                        cv = t + 1
                        if live(cv):
                            x_at = position_of(cv) - PAD
                            hold(sp, x_ordered, (cv - 1) * STEPS)
                            par = (k + 1) % 2
                            if t.least == UNITS - 2:
                                sp.dma_start(x_in[:, par, :, 0:XW - PAD],
                                             x_window(x_at, XW - PAD)).then_inc(x_loaded[par], 16)
                            else:
                                sp.dma_start(x_in[:, par, :, :],
                                             x_window(x_at, XW)).then_inc(x_loaded[par], 16)
                    if s == 0 and t.least < H // 2:
                        hold(sp, up_split, (t - 1) * 2)
                        load_up(t, k)
                    cv, _, _, q = units(t, s - 1)
                    if live(cv):
                        at = cv.now * (LC * 2 * ROW)
                        sp.wait_ge(y_done, (cv * STEPS + q + 1).now)
                        dst = bass.AP(y_dram.tensor, at + q * (COLS // N * J * 2 * ROW),
                                      [[N, P], [J * 2 * ROW, COLS // N], [1, N]])
                        sp.dma_start(dst, y_sb[:, q, :].rearrange("p (b n) -> p b n", n=N)).then_inc(y_stored[q], 16)
                    if s in (1, 3) and live(t - FIN_LAG + 1):
                        fin, half, par = t - FIN_LAG + 1, s // 2, (k + FIN_LAG + 1) % 2
                        z_at = fin.now * (LC * 2 * ROW) + half * ROW
                        x_at = position_of(fin) + half * (OH * L)
                        hold(sp, fin_done, (fin - 1) * STEPS - (STEPS - 2 * half - 2))
                        sp.wait_ge(scattered[half], ((fin // CHUNKS) * (16 * CHUNKS) + 16 * CHUNKS).now)
                        src = bass.AP(z_dram.tensor, z_at, [[2 * ROW, P], [1, ROW]])
                        sp.dma_start(zt_in[:, par, half, :, :].rearrange("p o n -> p (o n)"), src).then_inc(zt_loaded[par][half], 16)
                        hold(sp, out_stored[par][half], fin // 2 * 16)
                        src = bass.AP(x.tensor, x_at, [[C * L, N], [L, OH], [1, LC]])
                        sp.dma_start(x_res[:, par, half, :, :], src).then_inc(res_loaded[par][half], 16)

            pipeline(sp, iteration)
            for par in range(2):
                for half in range(2):
                    sp.wait_ge(out_stored[par][half], 16 * UNITS // 2)

        @block.gpsimd
        def _(pool):
            nc.gpsimd.memset(ident[:, :], 0.0).then_inc(ident_made, 1)
            pool.wait_ge(ident_made, 1)
            nc.gpsimd.affine_select(out=ident[:, :], in_=ident[:, :], compare_op=ALU.not_equal, fill=1.0, base=0,
                                    pattern=[[-1, P]], channel_multiplier=1).then_inc(ident_made, 1)

            def pass_waits():
                pool.sem_inc(pool_passed, 1)

            def iteration(t, k):
                cv, ffn, _, _ = units(t)
                if live(ffn - 1):
                    scatter(ffn - 1, (k + FFN_LAG + 1) % 2, 1)
                if live(cv + 1):
                    stage_conv(cv + 1, (k + 1) % 2)
                if live(ffn + 1):
                    par = (k + FFN_LAG + 1) % 2
                    stage_ffn(ffn + 1, par)
                    gather(ffn + 1, par, 0)
                if live(ffn):
                    scatter(ffn, (k + FFN_LAG) % 2, 0)
                if live(ffn + 1):
                    gather(ffn + 1, (k + FFN_LAG + 1) % 2, 1)

            def columns(flat, first, n):
                return flat[:, bass.ds(first, n)]

            def stage_conv(cv, par):
                W = 4 * P
                src = columns(conv_all[:, :, :, :, :].rearrange("p g a b m -> p (g a b m)"), (cv // CHUNKS).now * W, W)
                dst = conv_st[:, par, :, :, :].rearrange("p a b m -> p (a b m)")
                pool.wait_ge(prep_dve, 2)
                hold(pool, conv_done, (cv - 1) * STEPS)
                pass_waits()
                nc.gpsimd.tensor_copy(dst, src).then_inc(conv_staged, 1)

            def stage_ffn(ffn, par):
                pair = (ffn % CHUNKS).now
                W = 4 * M
                up_src = columns(up_all[:, :, :, :].rearrange("p h a m -> p (h a m)"), pair * W, W)
                W = 2 * KT * D
                down_src = columns(down_all[:, :, :, :].rearrange("p h k d -> p (h k d)"), pair * W, W)
                pool.wait_ge(up_split, H)
                hold(pool, down_done, (ffn - 1) * STEPS)
                pass_waits()
                nc.gpsimd.tensor_copy(up_st[:, par, :, :, :].rearrange("p h a m -> p (h a m)"), up_src)
                pool.wait_ge(down_loaded, 16)
                nc.gpsimd.tensor_copy(down_st[:, par, :, :, :].rearrange("p h k d -> p (h k d)"), down_src).then_inc(ffn_staged, 1)
                src = columns(rows_all[:, :, :].rearrange("p u w -> p (u w)"), ffn.now * 2, 2)
                pool.wait_ge(rows_made, 1)
                for half in range(2):
                    hold(pool, gathered[half], (ffn - 1) * 16)
                    hold(pool, scattered[half], (ffn - 1) * 16)
                pass_waits()
                nc.gpsimd.tensor_copy(rows[:, par, :], src).then_inc(rows_done, 1)

            def gather(ffn, par, half):
                hold(pool, rows_done, ffn + 1)
                for s in range(STEPS):
                    hold(pool, y_stored[s], (ffn // CHUNKS) * (16 * CHUNKS) + 16 * CHUNKS)
                hold(pool, t_split, ffn * STEPS - (STEPS - 2 * half - 2))
                pass_waits()
                table = y_dram[0:(ffn.least // CHUNKS + 1) * L * 2, :]
                nc.gpsimd.indirect_dma_start(
                    out=t_in[:, half, :], out_offset=None, in_=table,
                    in_offset=bass.IndirectOffsetOnAxis(ap=rows[:, par, half:half + 1], axis=0),
                ).then_inc(gathered[half], 16)

            def scatter(ffn, par, half):
                hold(pool, rows_done, ffn + 1)
                hold(pool, z_done, ffn * STEPS + 2 * half + 2)
                pass_waits()
                nc.gpsimd.indirect_dma_start(
                    out=z_dram, in_=z_sb[:, half, :], in_offset=None,
                    out_offset=bass.IndirectOffsetOnAxis(ap=rows[:, par, half:half + 1], axis=0),
                ).then_inc(scattered[half], 16)

            stage_conv(Count(0, 0), 0)
            pipeline(pool, iteration, by_group=True)

        @block.scalar
        def _(act):
            act.dma_start(c_row[:, :], cond).then_inc(ctx_loaded, 16)
            for j in range(J):
                act.dma_start(cw_rep[j * CO:(j + 1) * CO, :, :],
                              cond_w.rearrange("(g o) d -> o g d", g=G)).then_inc(ctx_loaded, 16)

            def iteration(t, k):
                for s in range(STEPS):
                    _, ffn, _, _ = units(t)
                    if live(ffn):
                        for head in range(2):
                            act.wait_ge(up_done, (ffn * (2 * STEPS) + 2 * s + head + 1).now)
                            hold(act, down_done, ffn * STEPS + s - 1)
                            nc.scalar.activation(h_sb[:, s % 2, head, :, :], ps[:, UP_BANK[head]:UP_BANK[head] + 2, :],
                                                 ACT.Gelu).then_inc(gelu_done, 1)
                    cv, _, _, q = units(t, s + 1)
                    if live(cv):
                        hi_part(cv, q)
                    _, ffn, fin, q = units(t, s - 1)
                    if live(ffn):
                        act.wait_ge(down_done, (ffn * STEPS + q + 1).now)
                        if q % 2 == 0:
                            hold(act, scattered[q // 2], ffn * 16)
                        nc.scalar.activation(z_sb[:, q // 2, (q % 2) * COLS:(q % 2 + 1) * COLS], down_ps,
                                             ACT.Copy).then_inc(z_done, 1)
                    cv, _, _, q2 = units(t, s + 2)
                    if live(cv):
                        order(cv, (k + (s + 2) // STEPS) % 2, q2)
                    if live(fin) and q % 2 == 1:
                        half, par = q // 2, (k + FIN_LAG + (s == 0)) % 2
                        act.wait_ge(sum_done, (fin * STEPS + q + 1).now)
                        dst = bass.AP(out.tensor, position_of(fin) + half * (OH * L), [[C * L, N], [L, OH], [1, LC]])
                        act.dma_start(dst, x_res[:, par, half, :, :]).then_inc(out_stored[par][half], 16)

            def hi_part(cv, s):
                act.wait_ge(xT_done, (cv * STEPS + s + 1).now)
                if s == 0:
                    nc.scalar.activation(xT_hi[:, 0, :], fin_ps[:, 0:N], ACT.Copy)
                nc.scalar.activation(xT_hi[:, 4 * s + 1:4 * s + 5, :].rearrange("p b n -> p (b n)"), xT_ps,
                                     ACT.Copy).then_inc(hi_done, 1)

            def order(cv, par, s):
                if s == 0:
                    act.wait_ge(x_loaded[par], ((cv // 2) * 16 + 16).now)
                hold(act, xT_done, cv * STEPS + s - 1)
                b = 0 if s == 0 else 1
                src = x_in[:, par, :, (4 * s + b) * J:(4 * s + 5) * J].rearrange("n i (b j) -> n b j i", j=J)
                dst = x_ord[:, s % 2, b:5, :].rearrange("n b (j i) -> n b j i", j=J)
                nc.scalar.activation(dst, src, ACT.Copy).then_inc(x_ordered, 1)

            act.wait_ge(pad_zero, 1)
            order(Count(0, 0), 0, 0)
            order(Count(0, 0), 0, 1)
            hi_part(Count(0, 0), 0)
            pipeline(act, iteration)

        @block.vector
        def _(dve):
            def lo_part(cv, s):
                dve.wait_ge(hi_done, (cv * STEPS + s + 1).now)

                def lo(b0, b1, src):
                    flat = "p b n -> p (b n)"
                    return nc.vector.tensor_tensor(xT_lo[:, b0:b1, :].rearrange(flat), src,
                                                   xT_hi[:, b0:b1, :].bitcast(F32).rearrange(flat), ALU.subtract)

                def zero_outside(rows, b, block_in_group):
                    def zero():
                        dve.wait_ge(lo_raw, ((cv * 2) + (1 if s == 0 else 2)).now)
                        nc.vector.memset(xT_hi[rows, b, :].bitcast(F32), 0.0)
                        nc.vector.memset(xT_lo[rows, b, :].bitcast(F32), 0.0)

                    place = (cv % CHUNKS).now
                    if isinstance(place, int):
                        if place == block_in_group:
                            zero()
                    else:
                        with dve.If(place == block_in_group):
                            zero()

                if s == 0:
                    lo(0, 1, fin_ps[:, 0:N]).then_inc(lo_raw, 1)
                    zero_outside(slice(0, PAD * CI), 0, 0)
                    lo(1, 5, xT_ps).then_inc(lo_done, 1)
                elif s == 3:
                    lo(NB, NB + 1, xT_ps[:, 3 * N:4 * N]).then_inc(lo_raw, 1)
                    zero_outside(slice(PAD * CI, P), NB, CHUNKS - 1)
                    lo(NB - 3, NB, xT_ps[:, 0:3 * N]).then_inc(lo_done, 1)
                else:
                    lo(4 * s + 1, 4 * s + 5, xT_ps).then_inc(lo_done, 1)

            def split(ffn, q):
                half, cols = q // 2, slice((q % 2) * COLS, (q % 2 + 1) * COLS)
                dve.wait_ge(gathered[half], (ffn * 16 + 16).now)
                hold(dve, up_done, ffn * (2 * STEPS) + 2 * q - 2)
                own = (slice(0, D), slice(D, P))
                for head in range(2):
                    nc.vector.tensor_copy(t_st[own[head], q % 2, head, :], t_in[own[head], half, cols]).then_inc(t_hi_done, 1)
                for head in range(2):
                    dve.wait_ge(t_hi_done, (ffn * (2 * STEPS) + 2 * q + head + 1).now)
                    last = nc.vector.tensor_tensor(t_st[own[1 - head], q % 2, head, :], t_in[own[head], half, cols],
                                                   t_st[own[head], q % 2, head, :].bitcast(F32), ALU.subtract)
                last.then_inc(t_split, 1)

            def split_up(pair, par):
                dve.wait_ge(up_loaded[par], (pair // 2 * 32 + 32).now)
                both = up_all[:, :, :, :].rearrange("p h a m -> p (h a m)")[:, bass.ds(pair.now * (4 * M), 4 * M)]
                both = both.rearrange("p (h a m) -> p h a m", h=2, a=2)
                nc.vector.tensor_copy(both[:, :, 0, :], up_raw[:, par, :, :]).then_inc(up_split, 1)
                dve.wait_ge(up_split, (pair * 2 + 1).now)
                nc.vector.tensor_tensor(both[:, :, 1, :], up_raw[:, par, :, :], both[:, :, 0, :].bitcast(F32),
                                        ALU.subtract).then_inc(up_split, 1)

            nc.vector.memset(x_in[:, 0, :, 0:PAD], 0.0).then_inc(pad_zero, 1)
            nc.vector.memset(tap_row[:, 0:J, :], 0.0)
            nc.vector.memset(tap_row[:, J + TAPS:3 * J, :], 0.0)
            dve.wait_ge(taps_loaded, 16)
            nc.vector.tensor_copy(tap_row[:, J:J + TAPS, :], tap_in[:, :, :].rearrange("c i t -> c t i")).then_inc(taps_laid, 1)
            dve.wait_ge(prep_pe, 1)
            for kt in range(2):
                src = ps[:, 2 * kt:2 * kt + 2, :].rearrange("p a w -> p (a w)")[:, 0:J * C]
                src = src.rearrange("p (j g o) -> p g j o", j=J, g=G)
                for g in range(G):
                    hi = conv_all[:, g, 0, kt, :].rearrange("p (j o) -> p j o", j=J)
                    last = nc.vector.tensor_copy(hi, src[:, g, :, :])
            last.then_inc(prep_dve, 1)
            dve.wait_ge(prep_dve, 1)
            for kt in range(2):
                src = ps[:, 2 * kt:2 * kt + 2, :].rearrange("p a w -> p (a w)")[:, 0:J * C]
                src = src.rearrange("p (j g o) -> p g j o", j=J, g=G)
                for g in range(G):
                    hi = conv_all[:, g, 0, kt, :].rearrange("p (j o) -> p j o", j=J)
                    lo = conv_all[:, g, 1, kt, :].rearrange("p (j o) -> p j o", j=J)
                    last = nc.vector.tensor_tensor(lo, src[:, g, :, :], hi.bitcast(F32), ALU.subtract)
            last.then_inc(prep_dve, 1)
            dve.wait_ge(prep_pe, 2)
            nc.vector.tensor_copy(cwT[:, :, :].rearrange("p g m -> p (g m)"), ps[:, 4, :])
            nc.vector.tensor_copy(cT[:, :], ps[:, 5, 0:N]).then_inc(prep_dve, 1)
            dve.wait_ge(prep_pe, 3)
            dve.wait_ge(bias_loaded, 16 * J)
            for g in range(G):
                last = nc.vector.tensor_scalar(ctx_bias[:, g, :], ps[:, 6, g * N:(g + 1) * N], bias_rep[:, g:g + 1], None,
                                               ALU.add)
            last.then_inc(prep_dve, 1)
            dve.wait_ge(perm_loaded, 16)
            for g in range(G):
                for half in range(2):
                    last = nc.vector.tensor_scalar(rows_all[:, g * CHUNKS:(g + 1) * CHUNKS, half], perm_sb[:, :],
                                                   2, 2 * g * L + half, ALU.mult, ALU.add)
            last.then_inc(rows_made, 1)
            lo_part(Count(0, 0), 0)

            def iteration(t, k):
                for s in range(STEPS):
                    cv, _, fin, q = units(t, s - 1)
                    if live(cv):
                        dve.wait_ge(conv_done, (cv * STEPS + q + 1).now)
                        hold(dve, y_stored[q], cv * 16)
                        at = (cv // CHUNKS).now * N
                        add = ctx_bias[:, :, :].rearrange("p g n -> p (g n)")[:, bass.ds(at, N)]
                        nc.vector.tensor_tensor(y_sb[:, q, :].rearrange("p (b n) -> p b n", n=N),
                                                conv_ps.rearrange("p (b n) -> p b n", n=N),
                                                add.unsqueeze(1).to_broadcast([P, COLS // N, N]),
                                                ALU.add).then_inc(y_done, 1)
                    if live(fin):
                        half, o, par = q // 2, 4 * (q % 2), (k + FIN_LAG + (s == 0)) % 2
                        dve.wait_ge(fin_done, (fin * STEPS + q + 1).now)
                        dve.wait_ge(res_loaded[par][half], (fin // 2 * 16 + 16).now)
                        here = x_res[:, par, half, o:o + 4, :]
                        nc.vector.tensor_tensor(here, fin_ps.rearrange("p (o l) -> p o l", l=LC), here,
                                                ALU.add).then_inc(sum_done, 1)
                    cv, ffn, _, q = units(t, s + 1)
                    if live(ffn):
                        split(ffn, q)
                    if live(cv):
                        lo_part(cv, q)
                    if s == 3 and t.least < H // 2:
                        split_up(t, k)

            pipeline(dve, iteration)

        @block.tensor
        def _(pe):
            pe.wait_ge(ident_made, 2)
            pe.wait_ge(taps_laid, 1)
            for kt in range(2):
                for j in range(J):
                    src = tap_row[:, (kt + 1) * J - j:(kt + 2) * J - j, :].rearrange("c t i -> c (t i)")
                    last = nc.tensor.transpose(ps[:, 2 * kt, j * C:(j + 1) * C], src, ident[0:C, 0:C])
            last.then_inc(prep_pe, 1)
            pe.wait_ge(ctx_loaded, 16 * (1 + J))
            for g in range(G):
                nc.tensor.transpose(ps[:, 4, g * P:(g + 1) * P], cw_rep[:, g, :], ident[:, :])
            nc.tensor.transpose(ps[:, 5, 0:N], c_row[:, :], ident[:, :]).then_inc(prep_pe, 1)
            pe.wait_ge(prep_dve, 3)
            for g in range(G):
                last = nc.tensor.matmul(ps[:, 6, g * N:(g + 1) * N], cwT[:, g, :], cT[:, :], start=True, stop=True)
            last.then_inc(prep_pe, 1)
            pe.wait_ge(prep_dve, 3)

            def transpose_x(cv, s):
                pe.wait_ge(x_ordered, (cv * STEPS + s + 1).now)
                hold(pe, lo_done, cv * STEPS + s)
                if s == 0:
                    nc.tensor.transpose(fin_ps[:, 0:N], x_ord[:, 0, 0, :], ident[:, :])
                for b in range(4):
                    last = nc.tensor.transpose(xT_ps[:, b * N:(b + 1) * N], x_ord[:, s % 2, b + 1, :], ident[:, :])
                last.then_inc(xT_done, 1)

            def up_project(ffn, par, s):
                if s == 0:
                    pe.wait_ge(ffn_staged, (ffn + 1).now)
                pe.wait_ge(t_split, (ffn * STEPS + s + 1).now)
                for head in range(2):
                    hold(pe, gelu_done, ffn * (2 * STEPS) + 2 * s + head - 1)
                    for kt in range(KT):
                        for part in range(2):
                            last = nc.tensor.matmul(ps[:, UP_BANK[head] + kt, :],
                                                    up_st[:, par, head, part, kt * P:(kt + 1) * P],
                                                    t_st[:, s % 2, head, :], start=part == 0, stop=part == 1)
                    last.then_inc(up_done, 1)

            def down_project(ffn, par, q):
                pe.wait_ge(gelu_done, (ffn * (2 * STEPS) + 2 * q + 2).now)
                hold(pe, z_done, ffn * STEPS + q)
                for kt in range(KT):
                    for head in range(2):
                        last = nc.tensor.matmul(down_ps[head * D:(head + 1) * D, :], down_st[:, par, head, kt, :],
                                                h_sb[:, q % 2, head, kt, :], start=kt == 0, stop=kt == KT - 1)
                last.then_inc(down_done, 1)

            def finish(fin, cv, par, s):
                half, o = s // 2, 4 * (s % 2)
                if s % 2 == 0:
                    pe.wait_ge(zt_loaded[par][half], (fin // 2 * 16 + 16).now)
                hold(pe, sum_done, fin * STEPS + s)
                if s == STEPS - 1 and live(cv + 1):
                    pe.wait_ge(lo_done, ((cv + 1) * STEPS + 1).now)
                for b in range(4):
                    last = nc.tensor.transpose(fin_ps[:, b * LC:(b + 1) * LC], zt_in[:, par, half, o + b, :], ident[:, :])
                last.then_inc(fin_done, 1)

            def convolve(cv, par, s):
                if s == 0:
                    pe.wait_ge(conv_staged, (cv + 1).now)
                pe.wait_ge(lo_done, (cv * STEPS + s + 1).now)
                hold(pe, y_done, cv * STEPS + s)
                terms = [(w, part, kt) for w, part in ((0, xT_hi), (0, xT_lo), (1, xT_hi)) for kt in range(2)]
                for n, (w, part, kt) in enumerate(terms):
                    last = nc.tensor.matmul(conv_ps, conv_st[:, par, w, kt, :],
                                            part[:, 4 * s + kt:4 * s + kt + 4, :].rearrange("p b n -> p (b n)"),
                                            start=n == 0, stop=n == len(terms) - 1)
                last.then_inc(conv_done, 1)

            def iteration(t, k):
                cv, ffn, fin, _ = units(t)
                for s in range(STEPS):
                    if live(ffn):
                        up_project(ffn, (k + FFN_LAG) % 2, s)
                    ahead, _, _, q = units(t, s + 1)
                    if live(ahead):
                        if q == 0 and live(fin):
                            pe.wait_ge(sum_done, (fin * STEPS + STEPS - 1).now)
                        transpose_x(ahead, q)
                    _, prev, _, q = units(t, s - 1)
                    if live(prev):
                        down_project(prev, (k + FFN_LAG + (s == 0)) % 2, q)
                    if live(fin):
                        finish(fin, cv, (k + FIN_LAG) % 2, s)
                    if live(cv):
                        convolve(cv, k, s)

            transpose_x(Count(0, 0), 0)
            pipeline(pe, iteration)


_OUT = ((128, 64, 1024), "float32")
_INS = ["x", "cond_128", "fside_S_0", "L0_cond_weight", "L0_cond_c_weight", "L0_ffn_up", "L0_ffn_down", "L0_ffn_perm"]


def kernel(**inputs):
    import numpy as _np
    import concourse.bacc as _bacc
    from concourse import mybir as _mybir
    from concourse.bass_utils import run_bass_kernel_spmd as _run

    nc = _bacc.Bacc("TRN2", target_bir_lowering=False, num_devices=1)
    arrays, args = {}, []
    for name in _INS:
        a = _np.ascontiguousarray(inputs[name])
        arrays[f"in_{name}"] = a
        args.append(nc.dram_tensor(f"in_{name}", a.shape, _mybir.dt.from_np(a.dtype), kind="ExternalInput").ap())
    shape, dtype = _OUT
    args.append(nc.dram_tensor("out_0", shape, _mybir.dt.from_np(_np.dtype(dtype)), kind="ExternalOutput").ap())
    adaln_ffn_kernel(nc, *args)
    r = _run(nc, [arrays], core_ids=[0])
    return r.results[0]["out_0"]
```

```python
import concourse.bass as bass
from concourse import mybir
from contextlib import ExitStack

F32 = mybir.dt.float32
F32R = mybir.dt.float32r
I32 = mybir.dt.int32
ALU = mybir.AluOpType
ACT = mybir.ActivationFunctionType


class Count:

    def __init__(self, now, least):
        self.now, self.least = now, least

    def __add__(self, k):
        return Count(self.now + k, self.least + k)

    def __sub__(self, k):
        return self + (-k)

    def __mul__(self, k):
        return Count(self.now * k, self.least * k)

    def __floordiv__(self, k):
        return Count(self.now // k, self.least // k)

    def __mod__(self, k):
        return Count(self.now % k, self.least % k)


def adaln_ffn_kernel(nc, x, cond, bias, conv_w, cond_w, up, down, perm, out):
    N, C, L = x.shape
    G, TAPS, CI = 4, conv_w.shape[2], conv_w.shape[1]
    CD = cond.shape[1]
    H, D, M = up.shape
    CO = C // G
    J = 8
    PAD = TAPS // 2
    P = 128
    LC = 128
    NB = LC // J
    XW = LC + J
    CHUNKS = L // LC
    UNITS = G * CHUNKS
    HALF = CHUNKS // 2
    STEPS = 4
    COLS = 512
    OH = CO // 2
    OQ = OH // 2
    ROW = OH * N
    KT = M // P
    FFN_LAG = CHUNKS + 2
    FIN_LAG = FFN_LAG + HALF + 1
    assert (N, C, CI, CO, M, D) == (P, G * CO, 16, 16, 2 * P, P // 2) and CHUNKS == 8 == H // 2

    y_dram = nc.dram_tensor("y_dram", [G * L * 2, ROW], F32, kind="Internal").ap()
    z_dram = nc.dram_tensor("z_dram", [G * L * 2, ROW], F32, kind="Internal").ap()

    ctx = ExitStack()
    with ctx:
        def sb(name, shape, dt=F32):
            return ctx.enter_context(nc.sbuf_tensor(name, shape, dt))

        def sem(name):
            return ctx.enter_context(nc.semaphore(name))

        ident = sb("ident", [P, P])
        tap_in = sb("tap_in", [C, CI, TAPS])
        tap_row = sb("tap_row", [C, 3 * J, CI])
        cw_rep = sb("cw_rep", [P, G, CD])
        cwT = sb("cwT", [P, G, P])
        c_row = sb("c_row", [N, CD])
        cT = sb("cT", [CD, N])
        bias_rep = sb("bias_rep", [P, G])
        ctx_bias = sb("ctx_bias", [P, G, N])
        conv_all = sb("conv_all", [P, G, 2, 2, P], F32R)
        conv_st = sb("conv_st", [P, 2, 2, 2, P], F32R)
        up_raw = sb("up_raw", [P, 2, 2, M])
        up_all = sb("up_all", [P, H, 2, M], F32R)
        up_st = sb("up_st", [P, 2, 2, 2, M], F32R)
        down_all = sb("down_all", [P, H, KT, D])
        down_st = sb("down_st", [P, 2, 2, KT, D])
        perm_sb = sb("perm_sb", [P, CHUNKS], I32)
        rows_all = sb("rows_all", [P, UNITS, 4], I32)
        from_rows = sb("from_rows", [P, 2, 2], I32)
        to_rows = sb("to_rows", [P, 2, 2], I32)
        x_in = sb("x_in", [N, 2, CI, XW])
        x_ord = sb("x_ord", [N, 2, 5, J * CI])
        xT_hi = sb("xT_hi", [P, NB + 1, N], F32R)
        xT_lo = sb("xT_lo", [P, NB + 1, N], F32R)
        y_sb = sb("y_sb", [P, STEPS, COLS])
        t_in = sb("t_in", [P, 2, 2, ROW])
        t_st = sb("t_st", [P, 2, 2, COLS], F32R)
        h_sb = sb("h_sb", [P, 2, 2, KT, COLS])
        z_sb = sb("z_sb", [P, 2, ROW])
        zt_in = sb("zt_in", [P, 2, 2, OH, N])
        x_res = sb("x_res", [N, 2, 2, OQ, 2 * LC])

        ps = ctx.enter_context(nc.psum_tensor("ps", [P, 8, COLS], F32))
        UP_BANK = (0, 2)
        down_ps, block0_ps = ps[:, 6, :], ps[:, 7, 0:N]

        def alone(cv):
            return cv.least < FFN_LAG

        def xT_ps(cv, s):
            return ps[:, UP_BANK[0] + 1 if alone(cv) and s % 2 else 4, :]

        def conv_ps(cv, s):
            return ps[:, 6 if alone(cv) and s % 2 else 5, :]


        taps_loaded, ctx_loaded, bias_loaded, perm_loaded = (
            sem(n) for n in ("taps_loaded", "ctx_loaded", "bias_loaded", "perm_loaded"))
        up_loaded = [sem(f"up_loaded{k}") for k in range(2)]
        down_loaded = [sem(f"down_loaded{q}") for q in range(HALF)]
        late_loaded = sem("late_loaded")
        ident_made, pad_zero = sem("ident_made"), sem("pad_zero")
        taps_turned, conv_hi_made, conv_made = sem("taps_turned"), sem("conv_hi_made"), sem("conv_made")
        ctx_turned, ctx_copied, ctx_done = sem("ctx_turned"), sem("ctx_copied"), sem("ctx_done")
        ctx_bias_made = sem("ctx_bias_made")
        taps_laid = sem("taps_laid")
        up_split, rows_made = sem("up_split"), sem("rows_made")
        x_loaded = [sem(f"x_loaded{k}") for k in range(2)]
        xT_done, hi_done, lo_done, lo_raw = sem("xT_done"), sem("hi_done"), sem("lo_done"), sem("lo_raw")
        x_ordered = sem("x_ordered")
        conv_done, y_done = sem("conv_done"), sem("y_done")
        y_stored = [sem(f"y_stored{s}") for s in range(STEPS)]
        conv_staged, up_staged, down_staged = sem("conv_staged"), sem("up_staged"), sem("down_staged")
        pool_passed = sem("pool_passed")
        from_rows_done, to_rows_done = sem("from_rows_done"), sem("to_rows_done")
        gathered = [[sem(f"gathered{par}{sub}") for sub in range(2)] for par in range(2)]
        t_hi_done, t_split = sem("t_hi_done"), sem("t_split")
        up_done, gelu_done, down_done, z_done = sem("up_done"), sem("gelu_done"), sem("down_done"), sem("z_done")
        scattered = [sem(f"scattered{k}") for k in range(2)]
        zt_loaded = [[sem(f"zt_loaded{par}{sub}") for sub in range(2)] for par in range(2)]
        res_loaded = [[sem(f"res_loaded{par}{sub}") for sub in range(2)] for par in range(2)]
        fin_done, sum_done = sem("fin_done"), sem("sum_done")
        out_stored = [[sem(f"out_stored{par}{sub}") for sub in range(2)] for par in range(2)]

        def hold(eng, what, count):
            if count.least > 0:
                eng.wait_ge(what, count.now)

        def units(t, s=0):
            return t + s // STEPS, t + (s // STEPS - FFN_LAG), t + (s // STEPS - FIN_LAG), s % STEPS

        def live(unit, least=0):
            return least <= unit.least < UNITS

        LAST = UNITS + FIN_LAG + 1

        def pipeline(eng, iteration, by_group=False, early=0, loops_end=None):
            def kind(i):
                t0 = 2 * i
                groups = tuple(by_group and (t0 + k - FFN_LAG + 1) // CHUNKS for k in range(2))
                stages = tuple(
                    min(max(t0 - lag, -4), 2) if t0 - lag < UNITS - 2 - ahead else min(t0 - lag, UNITS + 2)
                    for lag, ahead in ((0, early), ((FFN_LAG + 1) // 2 * 2, 0), (FIN_LAG, 0)))
                return groups, stages, max(t0, loops_end or FIN_LAG + UNITS - HALF - 1)

            i, end = 0, (LAST + 2) // 2
            while i < end:
                n = i + 1
                while n < end and kind(n) == kind(i):
                    n += 1
                if n - i == 1:
                    for k in range(2):
                        iteration(Count(2 * i + k, 2 * i + k), k)
                else:
                    with eng.Fori(i, n) as r:
                        for k in range(2):
                            iteration(Count(r * 2 + k, 2 * i + k), k)
                i = n

        def position_of(unit):
            return unit.now * LC + (unit // CHUNKS).now * (CO * L - L)

        def late(fin):
            return fin.least >= UNITS - HALF

        def residual(fin, par, quarter):
            if not late(fin):
                return x_res[:, par, quarter, :, :]
            at = 2 * (fin.least - (UNITS - HALF)) + quarter
            flat, first = ((x_in[:, :, :, :].rearrange("n a i w -> n (a i w)"), 0) if at < 4 else
                           (y_sb[:, :, :].rearrange("p s n -> p (s n)"), 4) if at < 6 else
                           (up_raw[:, :, :, :].rearrange("p a h m -> p (a h m)"), 6) if at < 7 else
                           (x_ord[:, :, :, :].rearrange("n a b w -> n (a b w)"), 7))
            at -= first
            return flat[:, at * OH * LC:(at + 1) * OH * LC].rearrange("n (o l) -> n o l", o=OQ)

        def fin_ps(fin, s):
            return ps[:, 4 if late(fin) and s % 2 else 7, :]

        def result_of(tensor, unit, quarter):
            first = unit.now * (2 * LC) + (unit // HALF).now * (OH * L - L) + quarter * (OQ * L)
            return bass.AP(tensor, first, [[C * L, N], [L, OQ], [1, 2 * LC]])

        block = ctx.enter_context(nc.Block())

        @block.sync
        def _(sp):
            def x_window(first, cols):
                return bass.AP(x.tensor, first, [[C * L, N], [L, CI], [1, cols]])

            def load_up(pair, par):
                src = up.rearrange("h d m -> (h d) m")[bass.ds(pair.now * P, P), :].rearrange("(h d) m -> d h m", d=D)
                for b in range(2):
                    sp.dma_start(up_raw[b * D:(b + 1) * D, par, :, :], src).then_inc(up_loaded[par], 16)

            def load_residual(fin, par, quarter, loaded):
                sp.dma_start(residual(fin, par, quarter), result_of(x.tensor, fin, quarter)).then_inc(loaded, 16)

            def load_block(fin, par, sub):
                hold(sp, fin_done, (fin - 1) * STEPS - (1 - sub))
                for b in range(2):
                    sp.wait_ge(scattered[b], ((fin // HALF) * (16 * HALF) + 16 * HALF).now)
                src = bass.AP(z_dram.tensor, fin.now * (2 * LC * ROW) + sub * (LC * ROW), [[ROW, P], [1, ROW]])
                sp.dma_start(zt_in[:, par, sub, :, :].rearrange("p o n -> p (o n)"), src).then_inc(zt_loaded[par][sub], 16)

            sp.dma_start(tap_in[:, :, :], conv_w).then_inc(taps_loaded, 16)
            sp.dma_start(x_in[:, 0, :, PAD:XW], x_window(0, XW - PAD)).then_inc(x_loaded[0], 16)
            with nc.allow_non_contiguous_dma(reason="small tables of the prologue"):
                for g in range(G):
                    sp.dma_start(bias_rep[:, g:g + 1],
                                 bass.AP(bias.tensor, g * CO, [[0, J], [1, CO], [1, 1]])).then_inc(bias_loaded, 16)
                sp.dma_start(x_in[:, 1, :, :], x_window(LC - PAD, XW)).then_inc(x_loaded[1], 16)
                sp.dma_start(perm_sb[:, :], perm.rearrange("(p d) -> d p", d=P)).then_inc(perm_loaded, 16)

            def iteration(t, k):
                for s in range(STEPS):
                    if s == 2:
                        cv = t + 2
                        if live(cv):
                            x_at = position_of(cv) - PAD
                            sp.wait_ge(x_ordered, ((cv - 1) * STEPS).now)
                            par = k
                            if cv.least == UNITS - 1:
                                sp.dma_start(x_in[:, par, :, 0:XW - PAD],
                                             x_window(x_at, XW - PAD)).then_inc(x_loaded[par], 16)
                            else:
                                sp.dma_start(x_in[:, par, :, :],
                                             x_window(x_at, XW)).then_inc(x_loaded[par], 16)
                    if s == 1 and 0 <= t.least - (FFN_LAG - 2) < HALF:
                        q, heads = t.least - (FFN_LAG - 2), H // HALF
                        src = down[q * heads:(q + 1) * heads, :, :].rearrange("h (k m) d -> m h k d", k=KT)
                        sp.dma_start(down_all[:, q * heads:(q + 1) * heads, :, :], src).then_inc(down_loaded[q], 16)
                    if s == 0 and t.least < H // 2:
                        hold(sp, up_split, (t - 1) * 2)
                        load_up(t, k)
                    cv, _, _, q = units(t, s - 1)
                    if live(cv):
                        at = cv.now * (LC * 2 * ROW)
                        sp.wait_ge(y_done, (cv * STEPS + q + 1).now)
                        dst = bass.AP(y_dram.tensor, at + q * (COLS // N * J * 2 * ROW),
                                      [[N, P], [J * 2 * ROW, COLS // N], [1, N]])
                        sp.dma_start(dst, y_sb[:, q, :].rearrange("p (b n) -> p b n", n=N)).then_inc(y_stored[q], 16)
                    fin, par = t - FIN_LAG + 1, (k + FIN_LAG + 1) % 2
                    if s in (1, 2) and live(fin):
                        load_block(fin, par, s - 1)
                    if s in (2, 3) and live(fin) and not late(fin):
                        hold(sp, out_stored[par][s - 2], fin // 2 * 16)
                        load_residual(fin, par, s - 2, res_loaded[par][s - 2])
                    if s == 3 and UNITS <= t.least < UNITS + 2 * HALF:
                        at = t.least - UNITS
                        sp.wait_ge(x_ordered, UNITS * STEPS)
                        sp.wait_ge(conv_done, UNITS * STEPS)
                        sp.wait_ge(up_split, H)
                        if at >= 4:
                            for q in range(STEPS):
                                sp.wait_ge(y_stored[q], 16 * UNITS)
                        fin = UNITS - HALF + at // 2
                        load_residual(Count(fin, fin), fin % 2, at % 2, late_loaded)

            pipeline(sp, iteration, early=2, loops_end=UNITS)
            for par in range(2):
                for sub in range(2):
                    sp.wait_ge(out_stored[par][sub], 16 * UNITS // 2)

        @block.gpsimd
        def _(pool):
            nc.gpsimd.memset(ident[:, :], 0.0).then_inc(ident_made, 1)
            pool.wait_ge(ident_made, 1)
            nc.gpsimd.affine_select(out=ident[:, :], in_=ident[:, :], compare_op=ALU.not_equal, fill=1.0, base=0,
                                    pattern=[[-1, P]], channel_multiplier=1).then_inc(ident_made, 1)

            def pass_waits():
                pool.sem_inc(pool_passed, 1)

            def iteration(t, k):
                if t.least < H // 2:
                    split_up(t, k)
                _, ffn, _, _ = units(t)
                par = (k + FFN_LAG) % 2
                if live(ffn + 1):
                    read_from(ffn + 1, 1 - par)
                    gather(ffn + 1, 1 - par, 0)
                if live(ffn - 1):
                    scatter(ffn - 1, 1 - par, 1)
                if live(ffn + 1):
                    gather(ffn + 1, 1 - par, 1)
                if live(ffn):
                    write_to(ffn, par)
                    scatter(ffn, par, 0)

            def split_up(pair, par):
                pool.wait_ge(up_loaded[par], (pair // 2 * 32 + 32).now)
                pass_waits()
                both = up_all[:, :, :, :].rearrange("p h a m -> p (h a m)")[:, bass.ds(pair.now * (4 * M), 4 * M)]
                both = both.rearrange("p (h a m) -> p h a m", h=2, a=2)
                nc.gpsimd.tensor_copy(both[:, :, 0, :], up_raw[:, par, :, :]).then_inc(up_split, 1)
                pool.wait_ge(up_split, (pair * 2 + 1).now)
                pass_waits()
                nc.gpsimd.tensor_tensor(both[:, :, 1, :], up_raw[:, par, :, :], both[:, :, 0, :].bitcast(F32),
                                        ALU.subtract).then_inc(up_split, 1)

            def rows_of(ffn, first):
                return rows_all[:, :, :].rearrange("p u w -> p (u w)")[:, bass.ds(ffn.now * 4 + first, 2)]

            def read_from(ffn, par):
                pool.wait_ge(rows_made, G)
                for sub in range(2):
                    hold(pool, gathered[par][sub], ffn // 2 * 16)
                pass_waits()
                nc.gpsimd.tensor_copy(from_rows[:, par, :], rows_of(ffn, 0)).then_inc(from_rows_done, 1)

            def write_to(ffn, par):
                for sub in range(2):
                    hold(pool, scattered[sub], (ffn - 1) * 16)
                pass_waits()
                nc.gpsimd.tensor_copy(to_rows[:, par, :], rows_of(ffn, 2)).then_inc(to_rows_done, 1)

            def gather(ffn, par, sub):
                hold(pool, from_rows_done, ffn + 1)
                for s in range(STEPS):
                    hold(pool, y_stored[s], (ffn // CHUNKS) * (16 * CHUNKS) + 16 * CHUNKS)
                hold(pool, t_split, (ffn - 1) * STEPS - (STEPS - 2 * sub - 2))
                pass_waits()
                table = y_dram[0:(ffn.least // CHUNKS + 1) * L * 2, :]
                nc.gpsimd.indirect_dma_start(
                    out=t_in[:, par, sub, :], out_offset=None, in_=table,
                    in_offset=bass.IndirectOffsetOnAxis(ap=from_rows[:, par, sub:sub + 1], axis=0),
                ).then_inc(gathered[par][sub], 16)

            def scatter(ffn, par, sub):
                hold(pool, to_rows_done, ffn + 1)
                hold(pool, z_done, ffn * STEPS + 2 * sub + 2)
                pass_waits()
                nc.gpsimd.indirect_dma_start(
                    out=z_dram, in_=z_sb[:, sub, :], in_offset=None,
                    out_offset=bass.IndirectOffsetOnAxis(ap=to_rows[:, par, sub:sub + 1], axis=0),
                ).then_inc(scattered[sub], 16)

            def rows_of_group(g):
                pool.wait_ge(perm_loaded, 16)
                for half in range(2):
                    u = (g * 2 + half) * HALF
                    for sub in range(2):
                        at = perm_sb[:, :].rearrange("p (q s) -> p q s", s=2)[:, :, sub]
                        nc.gpsimd.tensor_scalar(rows_all[:, u:u + HALF, sub], at, 2, 2 * g * L + half, ALU.mult, ALU.add)
                        last = nc.gpsimd.tensor_scalar(rows_all[:, u:u + HALF, 2 + sub], at, 1, (2 * g + half) * L,
                                                       ALU.mult, ALU.add)
                last.then_inc(rows_made, 1)

            for g in range(G):
                rows_of_group(g)
            pipeline(pool, iteration, by_group=True)

        @block.scalar
        def _(act):
            act.dma_start(c_row[:, :], cond).then_inc(ctx_loaded, 16)
            for g in range(G):
                act.dma_start(cw_rep[:, g, :],
                              bass.AP(cond_w.tensor, g * CO * CD, [[0, J], [CD, CO], [1, CD]])).then_inc(ctx_loaded, 16)

            def iteration(t, k):
                for s in range(STEPS):
                    _, ffn, _, _ = units(t)
                    if live(ffn):
                        for head in range(2):
                            act.wait_ge(up_done, (ffn * (2 * STEPS) + 2 * s + head + 1).now)
                            hold(act, down_done, ffn * STEPS + s - 1)
                            nc.scalar.activation(h_sb[:, s % 2, head, :, :], ps[:, UP_BANK[head]:UP_BANK[head] + 2, :],
                                                 ACT.Gelu).then_inc(gelu_done, 1)
                    coming, _, _, q2 = units(t, s + 2)
                    if live(coming) and alone(coming):
                        order(coming, (k + (s + 2) // STEPS) % 2, q2)
                    cv, _, _, q = units(t, s + 1)
                    if live(cv):
                        hi_part(cv, q)
                    _, ffn, fin, q = units(t, s - 1)
                    if live(ffn):
                        act.wait_ge(down_done, (ffn * STEPS + q + 1).now)
                        if q % 2 == 0:
                            hold(act, scattered[q // 2], ffn * 16)
                        nc.scalar.activation(z_sb[:, q // 2, (q % 2) * COLS:(q % 2 + 1) * COLS], down_ps,
                                             ACT.Copy).then_inc(z_done, 1)
                    if live(coming) and not alone(coming):
                        order(coming, (k + (s + 2) // STEPS) % 2, q2)
                    _, now, _, _ = units(t)
                    if s == 0 and live(now):
                        stage_up(now, 1)
                    if s == 2 and live(now + 1):
                        stage_up(now + 1, 0)
                    if live(fin) and q % 2 == 1:
                        quarter, par = q // 2, (k + FIN_LAG + (s == 0)) % 2
                        act.wait_ge(sum_done, (fin * STEPS + q + 1).now)
                        act.dma_start(result_of(out.tensor, fin, quarter),
                                      residual(fin, par, quarter)).then_inc(out_stored[par][quarter], 16)

            def stage_up(ffn, sub):
                act.wait_ge(up_split, H)
                hold(act, up_done, (ffn - 1) * (2 * STEPS) + 4 * (sub + 1))
                W = 4 * M
                src = up_all[:, :, :, :].rearrange("p h a m -> p (h a m)")[:, bass.ds((ffn % HALF).now * (2 * W) + sub * W, W)]
                nc.scalar.activation(up_st[:, sub, :, :, :].rearrange("p h a m -> p (h a m)"), src,
                                     ACT.Copy).then_inc(up_staged, 1)

            def hi_part(cv, s):
                act.wait_ge(xT_done, (cv * STEPS + s + 1).now)
                if s == 0:
                    nc.scalar.activation(xT_hi[:, 0, :], block0_ps, ACT.Copy)
                nc.scalar.activation(xT_hi[:, 4 * s + 1:4 * s + 5, :].rearrange("p b n -> p (b n)"), xT_ps(cv, s),
                                     ACT.Copy).then_inc(hi_done, 1)

            def order(cv, par, s):
                if s == 0:
                    act.wait_ge(x_loaded[par], ((cv // 2) * 16 + 16).now)
                hold(act, xT_done, cv * STEPS + s - 1)
                b = 0 if s == 0 else 1
                src = x_in[:, par, :, (4 * s + b) * J:(4 * s + 5) * J].rearrange("n i (b j) -> n b j i", j=J)
                dst = x_ord[:, s % 2, b:5, :].rearrange("n b (j i) -> n b j i", j=J)
                nc.scalar.activation(dst, src, ACT.Copy).then_inc(x_ordered, 1)

            act.wait_ge(pad_zero, 1)
            order(Count(0, 0), 0, 0)
            order(Count(0, 0), 0, 1)
            hi_part(Count(0, 0), 0)
            pipeline(act, iteration)

        @block.vector
        def _(dve):
            def lo_part(cv, s):
                dve.wait_ge(hi_done, (cv * STEPS + s + 1).now)

                def lo(b0, b1, src):
                    flat = "p b n -> p (b n)"
                    return nc.vector.tensor_tensor(xT_lo[:, b0:b1, :].rearrange(flat), src,
                                                   xT_hi[:, b0:b1, :].bitcast(F32).rearrange(flat), ALU.subtract)

                def zero_outside(rows, b, block_in_group):
                    def zero():
                        dve.wait_ge(lo_raw, ((cv * 2) + (1 if s == 0 else 2)).now)
                        nc.vector.memset(xT_hi[rows, b, :].bitcast(F32), 0.0)
                        nc.vector.memset(xT_lo[rows, b, :].bitcast(F32), 0.0)

                    place = (cv % CHUNKS).now
                    if isinstance(place, int):
                        if place == block_in_group:
                            zero()
                    else:
                        with dve.If(place == block_in_group):
                            zero()

                if s == 0:
                    lo(0, 1, block0_ps).then_inc(lo_raw, 1)
                    zero_outside(slice(0, PAD * CI), 0, 0)
                    lo(1, 5, xT_ps(cv, s)).then_inc(lo_done, 1)
                elif s == 3:
                    lo(NB, NB + 1, xT_ps(cv, s)[:, 3 * N:4 * N]).then_inc(lo_raw, 1)
                    zero_outside(slice(PAD * CI, P), NB, CHUNKS - 1)
                    lo(NB - 3, NB, xT_ps(cv, s)[:, 0:3 * N]).then_inc(lo_done, 1)
                else:
                    lo(4 * s + 1, 4 * s + 5, xT_ps(cv, s)).then_inc(lo_done, 1)

            def split(ffn, par, q):
                sub, cols = q // 2, slice((q % 2) * COLS, (q % 2 + 1) * COLS)
                dve.wait_ge(gathered[par][sub], (ffn // 2 * 16 + 16).now)
                hold(dve, up_done, ffn * (2 * STEPS) + 2 * q - 2)
                own = (slice(0, D), slice(D, P))
                for head in range(2):
                    nc.vector.tensor_copy(t_st[own[head], q % 2, head, :], t_in[own[head], par, sub, cols]).then_inc(t_hi_done, 1)
                for head in range(2):
                    dve.wait_ge(t_hi_done, (ffn * (2 * STEPS) + 2 * q + head + 1).now)
                    last = nc.vector.tensor_tensor(t_st[own[1 - head], q % 2, head, :], t_in[own[head], par, sub, cols],
                                                   t_st[own[head], q % 2, head, :].bitcast(F32), ALU.subtract)
                last.then_inc(t_split, 1)

            def stage_conv(cv, par):
                hold(dve, conv_done, (cv - 1) * STEPS)
                dve.wait_ge(conv_made, 1 if cv.least < 3 else G)
                W = 4 * P
                src = conv_all[:, :, :, :, :].rearrange("p g a b m -> p (g a b m)")[:, bass.ds((cv // CHUNKS).now * W, W)]
                nc.vector.tensor_copy(conv_st[:, par, :, :, :].rearrange("p a b m -> p (a b m)"), src).then_inc(conv_staged, 1)

            def stage_down(ffn, sub):
                for q in (range(2, HALF) if ffn.least >= 2 else [ffn.least]):
                    dve.wait_ge(down_loaded[q], 16)
                hold(dve, down_done, (ffn - 1) * STEPS + 2 * (sub + 1))
                W = 2 * KT * D
                src = down_all[:, :, :, :].rearrange("p h k d -> p (h k d)")[:, bass.ds((ffn % HALF).now * (2 * W) + sub * W, W)]
                nc.vector.tensor_copy(down_st[:, sub, :, :, :].rearrange("p h k d -> p (h k d)"), src).then_inc(down_staged, 1)

            nc.vector.memset(x_in[:, 0, :, 0:PAD], 0.0).then_inc(pad_zero, 1)
            nc.vector.memset(tap_row[:, 0:J, :], 0.0)
            nc.vector.memset(tap_row[:, J + TAPS:3 * J, :], 0.0)
            dve.wait_ge(taps_loaded, 16)
            nc.vector.tensor_copy(tap_row[:, J:J + TAPS, :], tap_in[:, :, :].rearrange("c i t -> c t i")).then_inc(taps_laid, 1)
            def conv_weights(g):
                def tile(kt, part):
                    src = ps[:, 2 * kt, 0:J * C].rearrange("p (j g o) -> p g j o", j=J, g=G)[:, g, :, :]
                    return src, conv_all[:, g, part, kt, :].rearrange("p (j o) -> p j o", j=J)
                dve.wait_ge(taps_turned, 1)
                for kt in range(2):
                    src, hi = tile(kt, 0)
                    last = nc.vector.tensor_copy(hi, src)
                last.then_inc(conv_hi_made, 1)
                dve.wait_ge(conv_hi_made, g + 1)
                for kt in range(2):
                    src, lo = tile(kt, 1)
                    last = nc.vector.tensor_tensor(lo, src, tile(kt, 0)[1].bitcast(F32), ALU.subtract)
                last.then_inc(conv_made, 1)

            conv_weights(0)
            stage_conv(Count(0, 0), 0)
            dve.wait_ge(ctx_turned, 1)
            nc.vector.tensor_copy(cwT[:, :, :].rearrange("p g m -> p (g m)"), ps[:, 3, :])
            nc.vector.tensor_copy(cT[:, :], ps[:, 6, 0:N]).then_inc(ctx_copied, 1)
            lo_part(Count(0, 0), 0)
            dve.wait_ge(ctx_done, 1)
            dve.wait_ge(bias_loaded, 16 * G)
            for g in range(G):
                last = nc.vector.tensor_scalar(ctx_bias[:, g, :], ps[:, 3, g * N:(g + 1) * N], bias_rep[:, g:g + 1], None,
                                               ALU.add)
            last.then_inc(ctx_bias_made, 1)

            def iteration(t, k):
                for s in range(STEPS):
                    cv, _, fin, q = units(t, s - 1)
                    if live(cv):
                        dve.wait_ge(conv_done, (cv * STEPS + q + 1).now)
                        hold(dve, y_stored[q], cv * 16)
                        dve.wait_ge(ctx_bias_made, 1)
                        at = (cv // CHUNKS).now * N
                        add = ctx_bias[:, :, :].rearrange("p g n -> p (g n)")[:, bass.ds(at, N)]
                        nc.vector.tensor_tensor(y_sb[:, q, :].rearrange("p (b n) -> p b n", n=N),
                                                conv_ps(cv, q).rearrange("p (b n) -> p b n", n=N),
                                                add.unsqueeze(1).to_broadcast([P, COLS // N, N]),
                                                ALU.add).then_inc(y_done, 1)
                    if live(fin):
                        quarter, sub, par = q // 2, q % 2, (k + FIN_LAG + (s == 0)) % 2
                        dve.wait_ge(fin_done, (fin * STEPS + q + 1).now)
                        if late(fin):
                            dve.wait_ge(late_loaded, 16 * 2 * HALF)
                        else:
                            dve.wait_ge(res_loaded[par][quarter], (fin // 2 * 16 + 16).now)
                        here = residual(fin, par, quarter)[:, :, sub * LC:(sub + 1) * LC]
                        nc.vector.tensor_tensor(here, fin_ps(fin, q).rearrange("p (o l) -> p o l", l=LC), here,
                                                ALU.add).then_inc(sum_done, 1)
                    cv, ffn, _, q = units(t, s + 1)
                    if live(ffn):
                        split(ffn, (k + FFN_LAG + (s == STEPS - 1)) % 2, q)
                    if live(cv):
                        lo_part(cv, q)
                    for g, turn in ((1, (0, 3)), (2, (1, 1)), (3, (1, 3))):
                        if (t.least, s) == turn:
                            conv_weights(g)
                    cv, ffn, _, _ = units(t)
                    if s == 1 and live(cv + 1):
                        stage_conv(cv + 1, (k + 1) % 2)
                    if s == 1 and live(ffn):
                        stage_down(ffn, 1)
                    if s == 3 and live(ffn + 1):
                        stage_down(ffn + 1, 0)

            pipeline(dve, iteration)

        @block.tensor
        def _(pe):
            pe.wait_ge(ident_made, 2)
            pe.wait_ge(taps_laid, 1)
            for kt in range(2):
                for j in range(J):
                    src = tap_row[:, (kt + 1) * J - j:(kt + 2) * J - j, :].rearrange("c t i -> c (t i)")
                    last = nc.tensor.transpose(ps[:, 2 * kt, j * C:(j + 1) * C], src, ident[0:C, 0:C])
            last.then_inc(taps_turned, 1)
            pe.wait_ge(ctx_loaded, 16 * (1 + G))
            for g in range(G):
                nc.tensor.transpose(ps[:, 3, g * P:(g + 1) * P], cw_rep[:, g, :], ident[:, :])
            nc.tensor.transpose(ps[:, 6, 0:N], c_row[:, :], ident[:, :]).then_inc(ctx_turned, 1)

            def transpose_x(cv, s):
                pe.wait_ge(x_ordered, (cv * STEPS + s + 1).now)
                hold(pe, lo_done, cv * STEPS + s - (1 if alone(cv) else 0))
                if s == 0:
                    nc.tensor.transpose(block0_ps, x_ord[:, 0, 0, :], ident[:, :])
                for b in range(4):
                    last = nc.tensor.transpose(xT_ps(cv, s)[:, b * N:(b + 1) * N], x_ord[:, s % 2, b + 1, :], ident[:, :])
                last.then_inc(xT_done, 1)

            def up_project(ffn, s):
                sub = s // 2
                if s % 2 == 0:
                    pe.wait_ge(up_staged, (ffn * 2 + sub + 1).now)
                pe.wait_ge(t_split, (ffn * STEPS + s + 1).now)
                for head in range(2):
                    hold(pe, gelu_done, ffn * (2 * STEPS) + 2 * s + head - 1)
                    for kt in range(KT):
                        for part in range(2):
                            last = nc.tensor.matmul(ps[:, UP_BANK[head] + kt, :],
                                                    up_st[:, sub, head, part, kt * P:(kt + 1) * P],
                                                    t_st[:, s % 2, head, :], start=part == 0, stop=part == 1)
                    last.then_inc(up_done, 1)

            def down_project(ffn, q):
                sub = q // 2
                if q % 2 == 0:
                    pe.wait_ge(down_staged, (ffn * 2 + sub + 1).now)
                pe.wait_ge(gelu_done, (ffn * (2 * STEPS) + 2 * q + 2).now)
                hold(pe, z_done, ffn * STEPS + q)
                for kt in range(KT):
                    for head in range(2):
                        last = nc.tensor.matmul(down_ps[head * D:(head + 1) * D, :], down_st[:, sub, head, kt, :],
                                                h_sb[:, q % 2, head, kt, :], start=kt == 0, stop=kt == KT - 1)
                last.then_inc(down_done, 1)

            def finish(fin, cv, par, s):
                quarter, sub = s // 2, s % 2
                if quarter == 0:
                    pe.wait_ge(zt_loaded[par][sub], (fin // 2 * 16 + 16).now)
                alternate = late(fin) and (s > 0 or late(fin - 1))
                hold(pe, sum_done, fin * STEPS + s - (1 if alternate else 0))
                if s == STEPS - 1 and live(cv + 1):
                    pe.wait_ge(lo_done, ((cv + 1) * STEPS + 1).now)
                for o in range(OQ):
                    last = nc.tensor.transpose(fin_ps(fin, s)[:, o * LC:(o + 1) * LC],
                                               zt_in[:, par, sub, quarter * OQ + o, :], ident[:, :])
                last.then_inc(fin_done, 1)

            def convolve(cv, par, s):
                if s == 0:
                    pe.wait_ge(conv_staged, (cv + 1).now)
                pe.wait_ge(lo_done, (cv * STEPS + s + 1).now)
                hold(pe, y_done, cv * STEPS + s - (1 if alone(cv) else 0))
                terms = [(w, part, kt) for w, part in ((0, xT_hi), (0, xT_lo), (1, xT_hi)) for kt in range(2)]
                for n, (w, part, kt) in enumerate(terms):
                    last = nc.tensor.matmul(conv_ps(cv, s), conv_st[:, par, w, kt, :],
                                            part[:, 4 * s + kt:4 * s + kt + 4, :].rearrange("p b n -> p (b n)"),
                                            start=n == 0, stop=n == len(terms) - 1)
                last.then_inc(conv_done, 1)

            def iteration(t, k):
                cv, ffn, fin, _ = units(t)
                for s in range(STEPS):
                    if live(ffn):
                        up_project(ffn, s)
                    ahead, _, _, q = units(t, s + 1)
                    if live(ahead):
                        if q == 0 and live(fin):
                            pe.wait_ge(sum_done, (fin * STEPS + STEPS - 1).now)
                        transpose_x(ahead, q)
                    _, prev, _, q = units(t, s - 1)
                    if live(prev):
                        down_project(prev, q)
                    if live(cv):
                        convolve(cv, k, s)
                    if live(fin):
                        finish(fin, cv, (k + FIN_LAG) % 2, s)

            transpose_x(Count(0, 0), 0)
            pe.wait_ge(ctx_copied, 1)
            for g in range(G):
                last = nc.tensor.matmul(ps[:, 3, g * N:(g + 1) * N], cwT[:, g, :], cT[:, :], start=True, stop=True)
            last.then_inc(ctx_done, 1)
            pipeline(pe, iteration)


_OUT = ((128, 64, 1024), "float32")
_INS = ["x", "cond_128", "fside_S_0", "L0_cond_weight", "L0_cond_c_weight", "L0_ffn_up", "L0_ffn_down", "L0_ffn_perm"]


def kernel(**inputs):
    import numpy as _np
    import concourse.bacc as _bacc
    from concourse import mybir as _mybir
    from concourse.bass_utils import run_bass_kernel_spmd as _run

    nc = _bacc.Bacc("TRN2", target_bir_lowering=False, num_devices=1)
    arrays, args = {}, []
    for name in _INS:
        a = _np.ascontiguousarray(inputs[name])
        arrays[f"in_{name}"] = a
        args.append(nc.dram_tensor(f"in_{name}", a.shape, _mybir.dt.from_np(a.dtype), kind="ExternalInput").ap())
    shape, dtype = _OUT
    args.append(nc.dram_tensor("out_0", shape, _mybir.dt.from_np(_np.dtype(dtype)), kind="ExternalOutput").ap())
    adaln_ffn_kernel(nc, *args)
    r = _run(nc, [arrays], core_ids=[0])
    return r.results[0]["out_0"]
```
